# Optimizing a Trainium2 kernel written in Bass

```python
import numpy as np
import jax
import jax.numpy as jnp

def _softmax(x, axis=-1):
    return jax.nn.softmax(x, axis=axis)

def _gelu(x):
    return jax.nn.gelu(x, approximate=True)

def _silu(x):
    return jax.nn.silu(x)

def _sigmoid(x):
    return jax.nn.sigmoid(x)

def _layernorm(x, axis=-1, eps=1e-05):
    m = jnp.mean(x, axis=axis, keepdims=True)
    v = jnp.var(x, axis=axis, keepdims=True)
    return (x - m) / jnp.sqrt(v + eps)

def _scatter_add(tgt, idx, src, axis=0):
    return tgt.at[idx].add(src)

def _segment_sum(src, seg, n):
    return jax.ops.segment_sum(src, seg, n)
kernel_name = 'mk_dlrm_tower_d1_rec_r8_0c36bf'

def setup_inputs(seed: int=0):
    np.random.seed(seed)
    _w = jnp.asarray

    def _rec_inputs():
        import jax
        import jax.numpy as jnp
        _tk = jax.random.key(seed)
        dense_ctx = jax.random.normal(jax.random.fold_in(_tk, 190), (2048, 16), jnp.float32)
        ids = jnp.stack([jax.random.randint(jax.random.fold_in(_tk, 200 + f), (2048,), 0, v, jnp.int32) for f, v in enumerate([12500, 1250, 1000, 1250, 12500, 125000, 125000, 125000, 1250, 1000, 12500, 1000, 1250, 12500, 1250, 1250])], axis=1)
        tbl_0 = 0.05 * jax.random.normal(jax.random.fold_in(_tk, 500 + 0), (12500, 16), jnp.float32)
        tbl_1 = 0.05 * jax.random.normal(jax.random.fold_in(_tk, 500 + 1), (1250, 16), jnp.float32)
        tbl_2 = 0.05 * jax.random.normal(jax.random.fold_in(_tk, 500 + 2), (1000, 16), jnp.float32)
        tbl_3 = 0.05 * jax.random.normal(jax.random.fold_in(_tk, 500 + 3), (1250, 16), jnp.float32)
        tbl_4 = 0.05 * jax.random.normal(jax.random.fold_in(_tk, 500 + 4), (12500, 16), jnp.float32)
        tbl_5 = 0.05 * jax.random.normal(jax.random.fold_in(_tk, 500 + 5), (125000, 16), jnp.float32)
        tbl_6 = 0.05 * jax.random.normal(jax.random.fold_in(_tk, 500 + 6), (125000, 16), jnp.float32)
        tbl_7 = 0.05 * jax.random.normal(jax.random.fold_in(_tk, 500 + 7), (125000, 16), jnp.float32)
        tbl_8 = 0.05 * jax.random.normal(jax.random.fold_in(_tk, 500 + 8), (1250, 16), jnp.float32)
        tbl_9 = 0.05 * jax.random.normal(jax.random.fold_in(_tk, 500 + 9), (1000, 16), jnp.float32)
        tbl_10 = 0.05 * jax.random.normal(jax.random.fold_in(_tk, 500 + 10), (12500, 16), jnp.float32)
        tbl_11 = 0.05 * jax.random.normal(jax.random.fold_in(_tk, 500 + 11), (1000, 16), jnp.float32)
        tbl_12 = 0.05 * jax.random.normal(jax.random.fold_in(_tk, 500 + 12), (1250, 16), jnp.float32)
        tbl_13 = 0.05 * jax.random.normal(jax.random.fold_in(_tk, 500 + 13), (12500, 16), jnp.float32)
        tbl_14 = 0.05 * jax.random.normal(jax.random.fold_in(_tk, 500 + 14), (1250, 16), jnp.float32)
        tbl_15 = 0.05 * jax.random.normal(jax.random.fold_in(_tk, 500 + 15), (1250, 16), jnp.float32)
        _rk = jax.random.fold_in(_tk, 7)
        r_x0 = -0.000233584 + 0.999828 * jax.random.normal(jax.random.fold_in(_rk, 101), (2048, 39, 16), jnp.float32)
        W_top1 = 0.0606339 * jax.random.normal(jax.random.fold_in(_tk, 801), (272, 512), jnp.float32)
        W_top2 = 0.0441942 * jax.random.normal(jax.random.fold_in(_tk, 802), (512, 256), jnp.float32)
        W_top3 = 0.0625 * jax.random.normal(jax.random.fold_in(_tk, 803), (256, 1), jnp.float32)
        b_top1 = jnp.zeros((512,), jnp.float32)
        b_top2 = jnp.zeros((256,), jnp.float32)
        return (dense_ctx, ids, tbl_0, tbl_1, tbl_2, tbl_3, tbl_4, tbl_5, tbl_6, tbl_7, tbl_8, tbl_9, tbl_10, tbl_11, tbl_12, tbl_13, tbl_14, tbl_15, r_x0, W_top1, b_top1, W_top2, b_top2, W_top3)
    dense_ctx, ids, tbl_0, tbl_1, tbl_2, tbl_3, tbl_4, tbl_5, tbl_6, tbl_7, tbl_8, tbl_9, tbl_10, tbl_11, tbl_12, tbl_13, tbl_14, tbl_15, r_x0, W_top1, b_top1, W_top2, b_top2, W_top3 = _rec_inputs()

    def _L0_rec_setup():
        import jax, jax.numpy as jnp
        import numpy as np
        B, S, F, D, K = (1024, 16, 39, 16, 16)
        key = jax.random.key(seed)
        k1, k2, k3, k4, k5 = jax.random.split(key, 5)
        xl = jax.random.normal(k1, (B, S, D), dtype=jnp.float32)
        x0 = jax.random.normal(k2, (B, F, D), dtype=jnp.float32)
        w = jnp.broadcast_to(jnp.eye(D, dtype=jnp.float32), (K, D, D)) + 0.02 * jax.random.normal(k3, (K, D, D), dtype=jnp.float32)
        alpha = jnp.ones((S * F, K), dtype=jnp.float32) + 0.02 * jax.random.normal(k4, (S * F, K), dtype=jnp.float32)
        hv = jnp.ones((K, D, 1), dtype=jnp.float32) + 0.02 * jax.random.normal(k5, (K, D, 1), dtype=jnp.float32)
        return {'xl': xl, 'x0': x0, 'w': w, 'alpha': alpha, 'hv': hv}
    _L0_rec_all = _L0_rec_setup()
    _L0_rec_in = {k: v for k, v in _L0_rec_all.items() if k in ('w', 'alpha', 'hv')}
    del _L0_rec_all
    return {'dense_ctx': dense_ctx, 'ids': ids, 'tbl_0': tbl_0, 'tbl_1': tbl_1, 'tbl_2': tbl_2, 'tbl_3': tbl_3, 'tbl_4': tbl_4, 'tbl_5': tbl_5, 'tbl_6': tbl_6, 'tbl_7': tbl_7, 'tbl_8': tbl_8, 'tbl_9': tbl_9, 'tbl_10': tbl_10, 'tbl_11': tbl_11, 'tbl_12': tbl_12, 'tbl_13': tbl_13, 'tbl_14': tbl_14, 'tbl_15': tbl_15, 'r_x0': r_x0, 'W_top1': W_top1, 'b_top1': b_top1, 'W_top2': W_top2, 'b_top2': b_top2, 'W_top3': W_top3, 'L0_rec_w': _L0_rec_in['w'], 'L0_rec_alpha': _L0_rec_in['alpha'], 'L0_rec_hv': _L0_rec_in['hv']}

def reference(dense_ctx, ids, tbl_0, tbl_1, tbl_2, tbl_3, tbl_4, tbl_5, tbl_6, tbl_7, tbl_8, tbl_9, tbl_10, tbl_11, tbl_12, tbl_13, tbl_14, tbl_15, r_x0, W_top1, b_top1, W_top2, b_top2, W_top3, L0_rec_w, L0_rec_alpha, L0_rec_hv):
    import jax
    import jax.numpy as jnp

    def _L0_rec_ref(xl, x0, w, alpha, hv):
        import jax, jax.numpy as jnp
        import numpy as np
        B, S, F, D, K = (1024, 16, 39, 16, 16)
        b, s, d = xl.shape
        f = x0.shape[1]
        A = jnp.repeat(x0, s, axis=1)
        Bm = jnp.repeat(xl, f, axis=2).reshape(b, s * f, d)
        out = jnp.einsum('bnh,bnd,nk,khd,kd->bkh', A, Bm, alpha, w, hv[..., 0])
        return out
    e = jnp.stack([tbl_0[ids[:, 0]], tbl_1[ids[:, 1]], tbl_2[ids[:, 2]], tbl_3[ids[:, 3]], tbl_4[ids[:, 4]], tbl_5[ids[:, 5]], tbl_6[ids[:, 6]], tbl_7[ids[:, 7]], tbl_8[ids[:, 8]], tbl_9[ids[:, 9]], tbl_10[ids[:, 10]], tbl_11[ids[:, 11]], tbl_12[ids[:, 12]], tbl_13[ids[:, 13]], tbl_14[ids[:, 14]], tbl_15[ids[:, 15]]], axis=1)
    z = _L0_rec_ref(e, r_x0, L0_rec_w, L0_rec_alpha, L0_rec_hv)
    z = z.reshape(z.shape[0], -1)
    h = jnp.concatenate([z, dense_ctx], axis=1)
    h = jnp.maximum(h @ W_top1 + b_top1, 0.0)
    h = jnp.maximum(h @ W_top2 + b_top2, 0.0)
    y = h @ W_top3
    return y

_drawn_inputs = setup_inputs


def setup_inputs(seed=0):
    import zlib

    import numpy as np

    out = dict(_drawn_inputs(seed))
    spreads = {'b_top1': (0.0, 0.1), 'b_top2': (0.0, 0.1)}
    factors = {}
    for name, (base, spread) in spreads.items():
        noise = np.random.default_rng([zlib.crc32(name.encode()), seed]).standard_normal(out[name].shape)
        drawn = base * np.exp(spread * noise) if base else spread * noise
        out[name] = jnp.asarray(drawn.astype(out[name].dtype))
    for name, factor in factors.items():
        out[name] = (out[name] * factor).astype(out[name].dtype)
    return out
```

```python
from contextlib import ExitStack

import numpy as np

import concourse.bass as bass
from concourse import mybir

F32 = mybir.dt.float32
F16 = mybir.dt.float16
BF16 = mybir.dt.bfloat16
I32 = mybir.dt.int32
ALU = mybir.AluOpType
ACT = mybir.ActivationFunctionType
AX_X = mybir.AxisListType.X

P = 128
VOCAB = [12500, 1250, 1000, 1250, 12500, 125000, 125000, 125000, 1250, 1000, 12500, 1000, 1250, 12500, 1250, 1250]
B, F, H, D, K = 2048, 39, 16, 16, 16
S = len(VOCAB)
E = S * D
REP = F
BLOCK = S * D
J = 8
ONE_HOT = [2, 9, 11, 1, 3, 8, 12, 14]
GATHERED = [s for s in range(S) if s not in ONE_HOT]
RC = 125
CHUNKS = [VOCAB[s] // RC for s in ONE_HOT]
CHUNK0 = [sum(CHUNKS[:n]) for n in range(len(ONE_HOT))]
NCHUNK = sum(CHUNKS)
PARTS = 3
TILES = B // P
GB = 256
TPG = GB // P
GROUPS = B // GB
HP = H // 2
FM = 32
MC = J // 2
NC = MC + 1
EXW = MC * P + P
XLP = (NC + 1) // 2
N1, N2 = 512, 256
DC = 16


def first_value(f):
    return BLOCK * f // REP


def spread_runs():
    runs = []
    for lo, hi in ((0, FM), (FM, F)):
        for odd in (0, 1):
            fs = list(range(lo + odd, hi, 2))
            while fs:
                n = 1
                while n < len(fs) and first_value(fs[n]) == first_value(fs[0]) + 13 * n:
                    n += 1
                n -= n > 1 and first_value(fs[n - 1]) + J > E
                width = min(J, E - first_value(fs[0]))
                runs.append((fs[0], n, first_value(fs[0]), width))
                fs = fs[n:]
    return runs


RUNS = spread_runs()


def shape_constants():
    e = np.arange(F * BLOCK).reshape(F, D, D)
    first = np.array([first_value(f) for f in range(F)])[:, None, None, None]
    slot = (e[:, :, None, :] // REP) == first + np.arange(J)[None, None, :, None]
    slot_mask = slot.transpose(1, 0, 2, 3).reshape(D, F * P).astype(np.float32)
    slot_block = (np.arange(P)[:, None] // D == np.arange(J)[None]).astype(np.float32)
    rows = np.arange(P)
    half = np.stack([rows // FM % 2 == 0, rows // FM % 2 == 1, rows // 64 == 0, rows // 64 == 1], 1)
    table_row = np.concatenate([np.arange(RC)[:, None] * c + np.arange(c) for c in CHUNKS], 1)
    return slot_mask, slot_block, half.astype(np.float32), table_row.astype(np.float32)


def dlrm_tower(nc, ids, ids_t, tables, x0_g, dense_t, alpha, w_t, hv_t, w1z, w1d, b1, w2, b2, w3,
               slot_mask, slot_block, row_half, table_row, y):
    with ExitStack() as ctx:
        def sb(name, shape, dt=F32):
            return ctx.enter_context(nc.sbuf_tensor(name, shape, dt))

        def sem(name):
            return ctx.enter_context(nc.semaphore(name))

        ident = sb("ident", [P, P])
        ids_sb = sb("ids_sb", [P, TILES, S], I32)
        e_all = sb("e_all", [P, TILES * E])
        spread = sb("spread", [P, 2, TPG, EXW])
        xl = sb("xl", [P, 2, NC, GB])
        x0_main = sb("x0_main", [P, 2, HP, GB])
        x0_last = sb("x0_last", [P, 2, HP, GB])
        prod = sb("prod", [P, NC, HP, GB])
        coef = sb("coef", [P, NC, HP, 2 * K])
        z_sb = sb("z_sb", [P, 2, 2, GB])
        h1_sb = sb("h1_sb", [P, N1 // P, GB])
        h2_sb = sb("h2_sb", [P, N2 // P, GB])
        y_sb = sb("y_sb", [1, B])
        dense_sb = sb("dense_sb", [DC + 1, B])
        w1z_sb = sb("w1z_sb", [P, 2, N1])
        w1d_sb = sb("w1d_sb", [DC + 1, N1])
        w2_sb = sb("w2_sb", [P, N1 // P, N2])
        b2_sb = sb("b2_sb", [P, N2 // P])
        w3_sb = sb("w3_sb", [P, N2 // P])
        half_sb = sb("half_sb", [P, 4])
        row_sb = sb("row_sb", [RC, NCHUNK])
        parts = sb("parts", [RC, NCHUNK, PARTS, D], BF16)
        ids_i = sb("ids_i", [RC, 2, B], I32)
        ids_h = sb("ids_h", [RC, 2, B], F16)
        onehot = sb("onehot", [RC, 2, B], BF16)
        alpha_sb = sb("alpha_sb", [D, F, K])
        wt_sb = sb("wt_sb", [P, K, H])
        hv_sb = sb("hv_sb", [P, K])
        wh_sb = sb("wh_sb", [P, K, H])
        block_sb = sb("block_sb", [P, J])
        bsum_sb = sb("bsum_sb", [P, F + 1, K])
        arena = prod[:, :, :, :].rearrange("p c h b -> p (c h b)")
        at = [0]

        def early(n):
            at[0] += n
            assert at[0] <= NC * HP * GB
            return arena[:, at[0] - n:at[0]]

        mask_sb = early(F * P)[0:D, :]
        wblock = early(K * J * H).rearrange("p (k j h) -> p k j h", k=K, j=J)
        blast = early(K * 8 * J).rearrange("p (k f j) -> p k f j", k=K, j=J)
        table_sb = early(NCHUNK * D)[0:RC, :].rearrange("p (c d) -> p c d", d=D)
        rest_sb = arena[0:RC, 0:NCHUNK * D].rearrange("p (c d) -> p c d", d=D)

        bank = [ctx.enter_context(nc.psum_tensor(f"bank{i}", [P, 512], F32)) for i in range(8)]
        z_ps = bank[0:2]
        t_ps = bank[2:4]
        h1_ps = bank[4:6]
        h2_ps = bank[6]
        y_ps = bank[7]
        look_ps = [bank[4:6], bank[6:8]]
        b_ps, c_ps, c4_ps = bank[0:2], bank[2], bank[3]

        prep_in = sem("prep_in")
        coef_in = sem("coef_in")
        table_in = sem("table_in")
        mlp_in = sem("mlp_in")
        pads_done = sem("pads_done")
        ident_done = sem("ident_done")
        ids_in = sem("ids_in")
        staged = [sem(f"staged{i}") for i in range(2)]
        ids_ready = sem("ids_ready")
        wh_done = sem("wh_done")
        bsum_done = sem("bsum_done")
        bsum_copied = sem("bsum_copied")
        lhs_done = sem("lhs_done")
        c_done = sem("c_done")
        coef_done = sem("coef_done")
        split_step = sem("split_step")
        onehot_ready = sem("onehot_ready")
        onehot_used = sem("onehot_used")
        looked_up = sem("looked_up")
        gathered = [sem(f"gathered{i}") for i in range(2)]
        x0_in = [sem(f"x0_in{i}") for i in range(2)]
        spread_ready = sem("spread_ready")
        transposed = sem("transposed")
        xl_ready = sem("xl_ready")
        product_ready = sem("product_ready")
        contracted = sem("contracted")
        z_ready = sem("z_ready")
        h1_summed = sem("h1_summed")
        h1_ready = sem("h1_ready")
        h2_summed = sem("h2_summed")
        h2_ready = sem("h2_ready")
        y_summed = sem("y_summed")
        y_ready = sem("y_ready")
        stored = sem("stored")

        PREP_LOADS, COEF_LOADS, TABLE_LOADS, MLP_LOADS, X0_LOADS = 2, 2 * J + 2, len(ONE_HOT) + 1, 6, 4

        def groups(eng, body):
            body(0, 0)
            with eng.Fori(0, (GROUPS - 2) // 2) as pair:
                for q in range(2):
                    body(pair * 2 + (1 + q), (1 + q) % 2)
            body(GROUPS - 1, (GROUPS - 1) % 2)

        block = ctx.enter_context(nc.Block())

        @block.sync
        def _(sp):
            sp.dma_start(mask_sb, slot_mask).then_inc(prep_in, 16)
            sp.dma_start(alpha_sb[:, :, :], alpha.rearrange("(f n) k -> n f k", n=D)).then_inc(prep_in, 16)
            for j in range(J):
                sp.dma_start(wt_sb[j * D:(j + 1) * D, :, :], w_t).then_inc(coef_in, 16)
                sp.dma_start(hv_sb[j * D:(j + 1) * D, :], hv_t).then_inc(coef_in, 16)
            sp.dma_start(block_sb[:, :], slot_block).then_inc(coef_in, 16)
            sp.dma_start(half_sb[:, :], row_half).then_inc(coef_in, 16)

            def load_x0(g, p):
                if not isinstance(g, int) or g >= 2:
                    sp.wait_ge(product_ready, NC * (g - 1))
                mine = x0_g[bass.ds(g, 1)]
                for j in range(2):
                    sp.dma_start(x0_main[64 * j:64 * j + 2 * FM, p, :, :],
                                 mine[0, :, 0:FM, :]).then_inc(x0_in[p], 16)
                for odd in range(2):
                    sp.dma_start(x0_last[64 * odd:64 * odd + (F - FM) * J, p, :, :],
                                 mine[0, odd, FM:F, :].unsqueeze(1).broadcast_to(
                                     [F - FM, J, HP * GB])).then_inc(x0_in[p], 16)

            sp.wait_ge(pads_done, 4)
            load_x0(0, 0)
            load_x0(1, 1)
            sp.dma_start(w1z_sb[:, :, :], w1z.rearrange("(a p) n -> p a n", p=P)).then_inc(mlp_in, 16)
            sp.dma_start(w1d_sb[0:DC, :], w1d).then_inc(mlp_in, 16)
            sp.dma_start(w1d_sb[DC:DC + 1, :], b1.rearrange("(a n) -> a n", a=1)).then_inc(mlp_in, 16)
            sp.dma_start(w2_sb[:, :, :], w2.rearrange("(a p) n -> p a n", p=P)).then_inc(mlp_in, 16)
            sp.dma_start(w3_sb[:, :], w3.rearrange("(a p) n -> p (a n)", p=P),
                         allow_slow_non_contiguous=True).then_inc(mlp_in, 16)
            sp.dma_start(dense_sb[0:DC, :], dense_t).then_inc(mlp_in, 16)
            with sp.Fori(1, GROUPS // 2) as pair:
                for p in range(2):
                    load_x0(pair * 2 + p, p)
            sp.wait_ge(y_ready, GROUPS)
            sp.dma_start(y.rearrange("b a -> a b"), y_sb[:, :]).then_inc(stored, 16)
            sp.wait_ge(stored, 16)

        @block.gpsimd
        def _(pool):
            pool.dma_start(ids_sb[:, :, :], ids.rearrange("(t p) s -> p t s", p=P)).then_inc(ids_in, 16)
            pool.memset(ident[:, :], 0.0).then_inc(ident_done, 1)
            pool.wait_ge(ident_done, 1)
            pool.affine_select(out=ident[:, :], in_=ident[:, :], compare_op=ALU.not_equal, fill=1.0, base=0,
                               pattern=[[-1, P]], channel_multiplier=1).then_inc(ident_done, 1)
            pool.wait_ge(ids_in, 16)
            per_group = 16 * TPG * len(GATHERED)
            for g in range(GROUPS):
                if g >= 2:
                    pool.wait_ge(gathered[g % 2], per_group * (g // 2))
                for t in range(g * TPG, (g + 1) * TPG):
                    for s in GATHERED:
                        pool.indirect_dma_start(
                            out=e_all[:, t * E + s * D:t * E + (s + 1) * D], out_offset=None,
                            in_=tables[s], in_offset=bass.IndirectOffsetOnAxis(ap=ids_sb[:, t, s:s + 1], axis=0),
                        ).then_inc(gathered[g % 2], 16)

        @block.scalar
        def _(act):
            act.dma_start(row_sb[:, :], table_row).then_inc(table_in, 16)

            def stage_ids(n):
                act.dma_start(ids_i[:, n % 2, :], ids_t[n:n + 1, :].broadcast_to([RC, B])).then_inc(staged[n % 2], 16)

            stage_ids(0)
            for n, s in enumerate(ONE_HOT):
                act.dma_start(table_sb[:, CHUNK0[n]:CHUNK0[n] + CHUNKS[n], :],
                              tables[s].rearrange("(p c) d -> p c d", p=RC)).then_inc(table_in, 16)
            stage_ids(1)
            act.dma_start(b2_sb[:, :], b2.rearrange("(a p) -> p a", p=P), allow_slow_non_contiguous=True).then_inc(mlp_in, 16)
            for n in range(len(ONE_HOT)):
                act.wait_ge(staged[n % 2], 16 * (n // 2 + 1))
                if n >= 2:
                    act.wait_ge(onehot_ready, CHUNK0[n - 1])
                act.activation(ids_h[:, n % 2, :], ids_i[:, n % 2, :], ACT.Copy).then_inc(ids_ready, 1)
                if n + 2 < len(ONE_HOT):
                    act.wait_ge(ids_ready, n + 1)
                    stage_ids(n + 2)

            def spread_group(g, p):
                if isinstance(g, int):
                    act.wait_ge(gathered[p], 16 * TPG * len(GATHERED) * (g // 2 + 1))
                else:
                    act.wait_ge(gathered[p], (g + (2 - p)) * (8 * TPG * len(GATHERED)))
                last = None
                for f0, count, i0, width in RUNS:
                    for odd in range(2):
                        src = window(g, i0, count, width)
                        if f0 < FM:
                            dst = spread[:, p, :, 0:MC * P].rearrange("p t (j h f) -> p t j h f", j=J, h=2)[
                                :, :, 0:width, odd, f0:f0 + 2 * count - 1:2]
                        else:
                            dst = spread[:, p, :, MC * P:EXW].rearrange("p t (h f j) -> p t h f j", h=2, f=8)[
                                :, :, odd, f0 - FM:f0 - FM + 2 * count - 1:2, 0:width].rearrange("p t f j -> p t j f")
                        last = act.activation(dst, src, ACT.Copy)
                last.then_inc(spread_ready, 1)

            def window(g, i0, count, width):
                first = e_all[:, bass.ds(g * (TPG * E) + i0, 1)]
                return bass.AP(first.tensor, first.offset, [list(first.ap[0]), [E, TPG], [1, width], [13, count]])

            def copy_xl(g, p):
                for i in range(XLP):
                    act.wait_ge(transposed, XLP * g + (i + 1))
                    n = min(2, NC - 2 * i)
                    act.activation(xl[:, p, 2 * i:2 * i + n, :],
                                   t_ps[(p + i) % 2][:, 0:n * GB].rearrange("p (a b) -> p a b", a=n),
                                   ACT.Copy).then_inc(xl_ready, 1)

            def finish_mlp(m):
                for i in range(2):
                    act.wait_ge(h1_summed, 2 * m + (i + 1))
                    act.activation(h1_sb[:, 2 * i:2 * i + 2, :],
                                   h1_ps[i][:, :].rearrange("p (a b) -> p a b", a=2), ACT.Relu).then_inc(h1_ready, 1)
                act.wait_ge(h2_summed, m + 1)
                for a in range(2):
                    act.activation(h2_sb[:, a, :], h2_ps[:, a * GB:(a + 1) * GB], ACT.Relu,
                                   bias=b2_sb[:, a:a + 1]).then_inc(h2_ready, 1)
                act.wait_ge(y_summed, m + 1)
                act.activation(y_sb[:, bass.ds(m * GB, GB)], y_ps[0:1, 0:GB], ACT.Copy).then_inc(y_ready, 1)

            def copy_z(g, p):
                act.wait_ge(contracted, NC * (g + 1))
                act.activation(z_sb[:, p, :, :], z_ps[p][:, :].rearrange("p (a b) -> p a b", a=2),
                               ACT.Copy).then_inc(z_ready, 1)

            act.wait_ge(looked_up, 2 * len(ONE_HOT))
            act.wait_ge(pads_done, 4)
            act.wait_ge(mlp_in, 16 * (MLP_LOADS + 1))
            spread_group(0, 0)

            def body(g, p):
                copy_xl(g, p)
                if not isinstance(g, int) or g > 0:
                    finish_mlp(g - 1)
                if not isinstance(g, int) or g < GROUPS - 1:
                    spread_group(g + 1, 1 - p)
                copy_z(g, p)

            groups(act, body)
            finish_mlp(GROUPS - 1)

        @block.vector
        def _(dve):
            dve.memset(x0_last[:, :, :, :], 0.0).then_inc(pads_done, 1)
            dve.memset(spread[:, :, :, :], 0.0).then_inc(pads_done, 1)
            dve.memset(bsum_sb[:, F:F + 1, :], 0.0).then_inc(pads_done, 1)
            dve.memset(dense_sb[:, :], 1.0).then_inc(pads_done, 1)
            dve.wait_ge(coef_in, 16 * COEF_LOADS)
            dve.tensor_tensor(wh_sb[:, :, :], wt_sb[:, :, :],
                              hv_sb[:, :].unsqueeze(2).broadcast_to([P, K, H]), ALU.mult).then_inc(wh_done, 1)
            dve.wait_ge(wh_done, 1)
            dve.tensor_tensor(wblock, wh_sb[:, :, :].unsqueeze(2).broadcast_to([P, K, J, H]),
                              block_sb[:, :].unsqueeze(1).unsqueeze(3).broadcast_to([P, K, J, H]),
                              ALU.mult).then_inc(lhs_done, 1)
            dve.wait_ge(bsum_done, 1)
            dve.tensor_copy(bsum_sb[:, 0:FM, :], b_ps[0][:, :].rearrange("p (f k) -> p f k", k=K)).then_inc(bsum_copied, 1)
            dve.tensor_copy(bsum_sb[:, FM:F, :],
                            b_ps[1][:, 0:(F - FM) * K].rearrange("p (f k) -> p f k", k=K)).then_inc(bsum_copied, 1)
            dve.wait_ge(bsum_copied, 2)
            dve.wait_ge(pads_done, 3)
            dve.tensor_tensor(blast,
                              bsum_sb[:, FM:F + 1, :].rearrange("p f k -> p k f").unsqueeze(3).broadcast_to([P, K, 8, J]),
                              block_sb[:, :].unsqueeze(1).unsqueeze(2).broadcast_to([P, K, 8, J]),
                              ALU.mult).then_inc(lhs_done, 1)
            dve.wait_ge(table_in, 16 * TABLE_LOADS)
            dve.tensor_copy(parts[:, :, 0, :], table_sb).then_inc(split_step, 1)
            dve.wait_ge(split_step, 1)
            dve.tensor_tensor(rest_sb, table_sb, parts[:, :, 0, :], ALU.subtract).then_inc(split_step, 1)
            dve.wait_ge(split_step, 2)
            dve.tensor_copy(parts[:, :, 1, :], rest_sb).then_inc(split_step, 1)
            dve.wait_ge(split_step, 3)
            dve.tensor_tensor(parts[:, :, 2, :], rest_sb, parts[:, :, 1, :], ALU.subtract).then_inc(split_step, 1)

            def make_onehot(n, slot, chunk):
                dve.tensor_scalar(onehot[:, slot, :], ids_h[:, n % 2, :], row_sb[:, bass.ds(chunk, 1)], None,
                                  ALU.is_equal).then_inc(onehot_ready, 1)

            def take_rows(n):
                dve.wait_ge(onehot_used, CHUNK0[n] + CHUNKS[n])
                s = ONE_HOT[n]
                for a in range(2):
                    dve.tensor_reduce(
                        e_all[:, :].rearrange("p (t i) -> p t i", i=E)[:, 8 * a:8 * a + 8, s * D:(s + 1) * D],
                        look_ps[n % 2][a][:, 0:8 * PARTS * D].rearrange("p (t c d) -> p t d c", t=8, c=PARTS),
                        AX_X, ALU.add).then_inc(looked_up, 1)

            for n in range(len(ONE_HOT)):
                dve.wait_ge(ids_ready, n + 1)
                for slot in range(2):
                    if n > 0:
                        dve.wait_ge(onehot_used, CHUNK0[n] + slot - 1)
                    make_onehot(n, slot, CHUNK0[n] + slot)
                with dve.Fori(1, CHUNKS[n] // 2) as pair:
                    for slot in range(2):
                        dve.wait_ge(onehot_used, pair * 2 + (CHUNK0[n] + slot - 1))
                        make_onehot(n, slot, pair * 2 + (CHUNK0[n] + slot))
                if n == 0:
                    dve.wait_ge(c_done, 1)
                    for h in range(2):
                        dve.tensor_scalar(
                            coef[:, 0:MC, :, h * K:(h + 1) * K].rearrange("p c a k -> p (c a) k"),
                            c_ps[:, :].rearrange("p (k c) -> p c k", k=K), half_sb[:, h:h + 1], None,
                            ALU.mult).then_inc(coef_done, 1)
                        dve.tensor_scalar(
                            coef[:, MC, :, h * K:(h + 1) * K],
                            c4_ps[:, 0:K * HP].rearrange("p (k a) -> p a k", k=K), half_sb[:, 2 + h:3 + h], None,
                            ALU.mult).then_inc(coef_done, 1)
                else:
                    take_rows(n - 1)
            take_rows(len(ONE_HOT) - 1)

            def body(g, p):
                if isinstance(g, int):
                    dve.wait_ge(x0_in[p], 16 * X0_LOADS * (g // 2 + 1))
                else:
                    dve.wait_ge(x0_in[p], (g + (2 - p)) * (8 * X0_LOADS))
                for c in range(NC):
                    dve.wait_ge(xl_ready, XLP * g + (c // 2 + 1))
                    if not isinstance(g, int) or g > 0:
                        dve.wait_ge(contracted, NC * (g - 1) + (c + 1))
                    x0 = x0_main if c < MC else x0_last
                    dve.tensor_tensor(prod[:, c, :, :], x0[:, p, :, :],
                                      xl[:, p, c, :].unsqueeze(1).broadcast_to([P, HP, GB]),
                                      ALU.mult).then_inc(product_ready, 1)

            groups(dve, body)

        @block.tensor
        def _(pe):
            pe.wait_ge(prep_in, 16 * PREP_LOADS)
            for f in range(F):
                last = pe.matmul(b_ps[f // FM][:, f % FM * K:(f % FM + 1) * K], mask_sb[:, f * P:(f + 1) * P],
                                 alpha_sb[:, f, :], start=True, stop=True)
            last.then_inc(bsum_done, 1)
            pe.wait_ge(bsum_copied, 2)
            pe.wait_ge(lhs_done, 2)
            for k in range(K):
                for j in range(2):
                    for odd in range(2):
                        row = 64 * j + 32 * odd
                        pe.matmul(c_ps[row:row + FM, k * MC * HP:(k + 1) * MC * HP], bsum_sb[:, 0:FM, k],
                                  wblock[:, k, j::2, odd::2], start=True, stop=True)
            for k in range(K):
                for odd in range(2):
                    last = pe.matmul(c4_ps[64 * odd:64 * odd + 64, k * HP:(k + 1) * HP],
                                     blast[:, k, :, :].rearrange("p f j -> p (f j)"),
                                     wh_sb[:, k, odd::2], start=True, stop=True)
            last.then_inc(c_done, 1)

            def look_up(n, slot, chunk, first, final):
                for t in range(TILES):
                    last = pe.matmul(look_ps[n % 2][t // 8][:, t % 8 * PARTS * D:(t % 8 + 1) * PARTS * D],
                                     onehot[:, slot, t * P:(t + 1) * P],
                                     parts[:, bass.ds(chunk, 1), :, :].rearrange("p a c d -> p (a c d)"),
                                     start=first and t % 8 == 0, stop=final, skip_group_check=True)
                last.then_inc(onehot_used, 1)

            pe.wait_ge(split_step, 4)
            for n in range(len(ONE_HOT)):
                if n >= 2:
                    pe.wait_ge(looked_up, 2 * (n - 1))
                for slot in range(2):
                    pe.wait_ge(onehot_ready, CHUNK0[n] + slot + 1)
                    look_up(n, slot, CHUNK0[n] + slot, slot == 0, False)
                with pe.Fori(1, CHUNKS[n] // 2) as pair:
                    for slot in range(2):
                        pe.wait_ge(onehot_ready, pair * 2 + (CHUNK0[n] + slot + 1))
                        look_up(n, slot, pair * 2 + (CHUNK0[n] + slot), False, False)

            def transpose_values(g, p):
                pe.wait_ge(spread_ready, g + 1)
                for i in range(XLP):
                    if not isinstance(g, int) or g > 0 or i >= 2:
                        pe.wait_ge(xl_ready, XLP * g + (i - 1))
                    for c in range(2 * i, min(2 * i + 2, NC)):
                        for t in range(TPG):
                            col = c % 2 * GB + t * P
                            last = pe.transpose(t_ps[(p + i) % 2][:, col:col + P],
                                                spread[:, p, t, c * P:(c + 1) * P], ident[:, :])
                    last.then_inc(transposed, 1)

            def contract(g, p, c):
                pe.wait_ge(product_ready, NC * g + (c + 1))
                for a in range(2):
                    for q in range(4):
                        last = pe.matmul(z_ps[p][32 * q:32 * q + 32, a * GB:(a + 1) * GB], coef[:, c, 4 * a + q, :],
                                         prod[:, c, 4 * a + q, :], start=(c == 0 and a == 0), stop=(c == NC - 1),
                                         skip_group_check=True)
                last.then_inc(contracted, 1)

            def layer1(m, p, i):
                for a in range(2):
                    out = h1_ps[i][:, a * GB:(a + 1) * GB]
                    cols = slice((2 * i + a) * P, (2 * i + a + 1) * P)
                    pe.matmul(out, w1d_sb[:, cols], dense_cols(m), start=True, stop=False)
                    pe.matmul(out, w1z_sb[:, 0, cols], z_sb[:, p, 0, :], start=False, stop=False)
                    last = pe.matmul(out, w1z_sb[:, 1, cols], z_sb[:, p, 1, :], start=False, stop=True)
                last.then_inc(h1_summed, 1)

            def dense_cols(m):
                return dense_sb[:, bass.ds(m * GB, GB)]

            def layer2(m):
                pe.wait_ge(h1_ready, 2 * m + 2)
                for a in range(2):
                    for c in range(N1 // P):
                        last = pe.matmul(h2_ps[:, a * GB:(a + 1) * GB], w2_sb[:, c, a * P:(a + 1) * P],
                                         h1_sb[:, c, :], start=(c == 0), stop=(c == N1 // P - 1))
                last.then_inc(h2_summed, 1)

            def layer3(m):
                pe.wait_ge(h2_ready, 2 * m + 2)
                for a in range(2):
                    last = pe.matmul(y_ps[0:1, 0:GB], w3_sb[:, a:a + 1], h2_sb[:, a, :], start=(a == 0), stop=(a == 1))
                last.then_inc(y_summed, 1)

            pe.wait_ge(ident_done, 2)
            pe.wait_ge(coef_done, 4)
            pe.wait_ge(mlp_in, 16 * (MLP_LOADS + 1))
            pe.wait_ge(looked_up, 2 * len(ONE_HOT))

            def body(g, p):
                transpose_values(g, p)
                before = not isinstance(g, int) or g > 0
                for c in range(NC):
                    contract(g, p, c)
                    if before and c == 0:
                        pe.wait_ge(z_ready, g)
                    if before and c < 2:
                        layer1(g - 1, 1 - p, c)
                    if before and c == 3:
                        layer2(g - 1)
                if before:
                    layer3(g - 1)

            groups(pe, body)
            pe.wait_ge(z_ready, GROUPS)
            m, p = GROUPS - 1, (GROUPS - 1) % 2
            layer1(m, p, 0)
            layer1(m, p, 1)
            layer2(m)
            layer3(m)


def kernel(dense_ctx, ids, r_x0, W_top1, b_top1, W_top2, b_top2, W_top3, L0_rec_w, L0_rec_alpha, L0_rec_hv, **tables):
    import numpy as _np
    import concourse.bacc as _bacc
    from concourse import mybir as _mybir
    from concourse.bass_utils import run_bass_kernel_spmd as _run

    flat = lambda a: _np.ascontiguousarray(_np.asarray(a))
    ids, w1, hv = flat(ids), flat(W_top1), flat(L0_rec_hv)
    slot_mask, slot_block, row_half, table_row = shape_constants()
    arrays = {
        "ids": ids,
        "ids_t": flat(ids[:, ONE_HOT].T),
        **{f"tbl_{s}": flat(tables[f"tbl_{s}"]) for s in range(S)},
        "x0_g": flat(flat(r_x0).reshape(GROUPS, GB, F, HP, 2).transpose(0, 4, 2, 3, 1).reshape(GROUPS, 2, F, HP * GB)),
        "dense_t": flat(flat(dense_ctx).T),
        "alpha": flat(L0_rec_alpha),
        "w_t": flat(flat(L0_rec_w).transpose(2, 0, 1)),
        "hv_t": flat(hv[:, :, 0].T),
        "w1z": flat(w1[:K * H].reshape(K, H, N1).transpose(1, 0, 2).reshape(K * H, N1)),
        "w1d": flat(w1[K * H:]),
        "b1": flat(b_top1),
        "w2": flat(W_top2),
        "b2": flat(b_top2),
        "w3": flat(W_top3),
        "slot_mask": slot_mask,
        "slot_block": slot_block,
        "row_half": row_half,
        "table_row": table_row,
    }
    nc = _bacc.Bacc("TRN2", target_bir_lowering=False, num_devices=1)
    aps = {n: nc.dram_tensor(n, a.shape, _mybir.dt.from_np(a.dtype), kind="ExternalInput").ap() for n, a in arrays.items()}
    table_aps = [aps.pop(f"tbl_{s}") for s in range(S)]
    y = nc.dram_tensor("y", (B, 1), _mybir.dt.float32, kind="ExternalOutput").ap()
    dlrm_tower(nc, tables=table_aps, y=y, **aps)
    return _run(nc, [arrays], core_ids=[0]).results[0]["y"]
```

```python
from contextlib import ExitStack

import numpy as np

import concourse.bass as bass
from concourse import mybir

F32 = mybir.dt.float32
F16 = mybir.dt.float16
BF16 = mybir.dt.bfloat16
I32 = mybir.dt.int32
ALU = mybir.AluOpType
ACT = mybir.ActivationFunctionType
AX_X = mybir.AxisListType.X

P = 128
VOCAB = [12500, 1250, 1000, 1250, 12500, 125000, 125000, 125000, 1250, 1000, 12500, 1000, 1250, 12500, 1250, 1250]
B, F, H, D, K = 2048, 39, 16, 16, 16
S = len(VOCAB)
E = S * D
REP = F
BLOCK = S * D
J = 8
ONE_HOT = [2, 9, 11, 1, 3, 8, 12]
GATHERED = [s for s in range(S) if s not in ONE_HOT]
RC = 125
CHUNKS = [VOCAB[s] // RC for s in ONE_HOT]
CHUNK0 = [sum(CHUNKS[:n]) for n in range(len(ONE_HOT))]
NCHUNK = sum(CHUNKS)
PARTS = 3
TILES = B // P
GB = 256
TPG = GB // P
SLOTS = 3
GROUPS = B // GB
HP = H // 2
F8 = -(-F // 8)
FM = 32
MC = J // 2
NC = MC + 1
EXW = MC * P + P
XLP = (NC + 1) // 2
N1, N2 = 512, 256
DC = 16


def first_value(f):
    return BLOCK * f // REP


def spread_runs():
    runs = []
    for lo, hi in ((0, FM), (FM, F)):
        for odd in (0, 1):
            fs = list(range(lo + odd, hi, 2))
            while fs:
                n = 1
                while n < len(fs) and first_value(fs[n]) == first_value(fs[0]) + 13 * n:
                    n += 1
                n -= n > 1 and first_value(fs[n - 1]) + J > E
                width = min(J, E - first_value(fs[0]))
                runs.append((fs[0], n, first_value(fs[0]), width))
                fs = fs[n:]
    return runs


RUNS = spread_runs()


def shape_constants():
    e = np.arange(F * BLOCK).reshape(F, D, D)
    first = np.array([first_value(f) for f in range(F)])[:, None, None, None]
    slot = (e[:, :, None, :] // REP) == first + np.arange(J)[None, None, :, None]
    slot_mask = np.zeros((F8 * 8, D, P), np.float32)
    slot_mask[0:F] = slot.reshape(F, D, P)
    slot_mask = slot_mask.reshape(F8, P, P).transpose(1, 0, 2).reshape(P, F8 * P)
    slot_block = (np.arange(P)[:, None] // D == np.arange(J)[None]).astype(np.float32)
    rows = np.arange(P)
    half = np.stack([rows // FM % 2 == 0, rows // FM % 2 == 1, rows // 64 == 0, rows // 64 == 1], 1)
    table_row = np.concatenate([np.arange(P)[:, None] * c + np.arange(c) for c in CHUNKS], 1)
    return slot_mask, np.concatenate([slot_block, half, table_row], 1).astype(np.float32)


def dlrm_tower(nc, ids, ids_t, small_tables, tables, x0_g, dense_t, alpha, w_hv, w1z, w1d, w2, b2, w3,
               slot_mask, masks, y):
    with ExitStack() as ctx:
        def sb(name, shape, dt=F32):
            return ctx.enter_context(nc.sbuf_tensor(name, shape, dt))

        def sem(name):
            return ctx.enter_context(nc.semaphore(name))

        ident = sb("ident", [P, P])
        ids_sb = sb("ids_sb", [P, TILES, S], I32)
        e_all = sb("e_all", [P, TILES * E])
        spread = sb("spread", [P, 2, TPG, EXW])
        xl = sb("xl", [P, 2, NC, GB])
        x0_main = sb("x0_main", [P, 2, HP, GB])
        x0_last = sb("x0_last", [P, 2, HP, GB])
        prod = sb("prod", [P, NC, HP, GB])
        coef = sb("coef", [P, NC, HP, 2 * K])
        z_sb = sb("z_sb", [P, 2, 2, GB])
        h1_sb = sb("h1_sb", [P, N1 // P, GB])
        h2_sb = sb("h2_sb", [P, N2 // P, GB])
        y_sb = sb("y_sb", [1, B])
        dense_sb = sb("dense_sb", [DC + 1, B])
        w1z_sb = sb("w1z_sb", [P, 2, N1])
        w1d_sb = sb("w1d_sb", [DC + 1, N1])
        w2_sb = sb("w2_sb", [P, N1 // P, N2])
        b2_sb = sb("b2_sb", [P, N2 // P])
        w3_sb = sb("w3_sb", [P, N2 // P])
        masks_sb = sb("masks_sb", [P, J + 4 + NCHUNK])
        block_sb, half_sb, row_sb = masks_sb[:, 0:J], masks_sb[:, J:J + 4], masks_sb[0:RC, J + 4:J + 4 + NCHUNK]
        parts = sb("parts", [RC, NCHUNK, PARTS, D], BF16)
        ids_i = sb("ids_i", [RC, 2, B], I32)
        ids_h = sb("ids_h", [RC, 2, B], F16)
        onehot = sb("onehot", [RC, SLOTS, B], BF16)
        alpha_sb = sb("alpha_sb", [P, F8, K])
        w_hv_sb = sb("w_hv_sb", [P, K * H + K])
        wh_sb = sb("wh_sb", [P, K, H])
        bsum_sb = sb("bsum_sb", [P, F + 1, K])
        arena = prod[:, :, :, :].rearrange("p c h b -> p (c h b)")
        at = [0]

        def early(n):
            at[0] += n
            assert at[0] <= NC * HP * GB
            return arena[:, at[0] - n:at[0]]

        mask_sb = early(F8 * P)
        alpha_block = early(F8 * 8 * K).rearrange("p (c f k) -> p c f k", c=F8, f=8)
        wblock = early(K * J * H).rearrange("p (k j h) -> p k j h", k=K, j=J)
        blast = early(K * 2 * 8 * J).rearrange("p (k h f j) -> p k h f j", k=K, h=2, j=J)
        table_sb = early(NCHUNK * D)[0:RC, :].rearrange("p (c d) -> p c d", d=D)
        rest_sb = early(NCHUNK * D)[0:RC, :].rearrange("p (c d) -> p c d", d=D)

        bank = [ctx.enter_context(nc.psum_tensor(f"bank{i}", [P, 512], F32)) for i in range(8)]
        z_ps = bank[0:2]
        t_ps = bank[2:4]
        h1_ps = bank[4:6]
        h2_ps = bank[6]
        y_ps = bank[7]
        look_ps = [bank[4:6], bank[6:8]]
        b_ps, c_ps, c4_ps = bank[0:2], bank[2], bank[3]

        prep_in = sem("prep_in")
        masks_in = sem("masks_in")
        coef_in = sem("coef_in")
        table_in = sem("table_in")
        mlp_in = sem("mlp_in")
        pads_done = sem("pads_done")
        ident_done = sem("ident_done")
        ids_in = sem("ids_in")
        staged = [sem(f"staged{i}") for i in range(2)]
        ids_ready = sem("ids_ready")
        wh_done = sem("wh_done")
        alpha_spread = sem("alpha_spread")
        bsum_done = sem("bsum_done")
        bsum_copied = sem("bsum_copied")
        lhs_done = sem("lhs_done")
        c_done = sem("c_done")
        coef_done = sem("coef_done")
        split_step = sem("split_step")
        onehot_ready = sem("onehot_ready")
        onehot_used = sem("onehot_used")
        looked_up = sem("looked_up")
        gathered = [sem(f"gathered{i}") for i in range(2)]
        x0_in = [sem(f"x0_in{i}") for i in range(2)]
        spread_ready = sem("spread_ready")
        transposed = sem("transposed")
        xl_ready = sem("xl_ready")
        product_ready = sem("product_ready")
        contracted = sem("contracted")
        z_ready = sem("z_ready")
        h1_summed = sem("h1_summed")
        h1_ready = sem("h1_ready")
        h2_summed = sem("h2_summed")
        h2_ready = sem("h2_ready")
        y_summed = sem("y_summed")
        y_ready = sem("y_ready")
        stored = sem("stored")

        PREP_LOADS, MLP_LOADS, X0_LOADS = 2, 6, 4

        def groups(eng, body):
            for g in (0, 1):
                body(g, g % 2)
            with eng.Fori(1, GROUPS // 2 - 1) as pair:
                for p in range(2):
                    body(pair * 2 + p, p)
            for g in (GROUPS - 2, GROUPS - 1):
                body(g, g % 2)

        block = ctx.enter_context(nc.Block())

        @block.sync
        def _(sp):
            sp.dma_start(masks_sb[:, :], masks).then_inc(masks_in, 16)
            sp.dma_start(table_sb, small_tables.rearrange("p (c d) -> p c d", d=D)).then_inc(table_in, 16)
            sp.dma_start(mask_sb, slot_mask).then_inc(prep_in, 16)
            sp.dma_start(alpha_sb[:, :, :], alpha.rearrange("(c p) k -> p c k", p=P)).then_inc(prep_in, 16)
            sp.dma_start(w_hv_sb[:, :], w_hv.unsqueeze(0).broadcast_to([J, D, K * H + K])).then_inc(coef_in, 16)

            def load_x0(g, p):
                if not isinstance(g, int) or g >= 2:
                    sp.wait_ge(product_ready, NC * (g - 1))
                mine = x0_g[bass.ds(g, 1)]
                for j in range(2):
                    sp.dma_start(x0_main[64 * j:64 * j + 2 * FM, p, :, :],
                                 mine[0, :, 0:FM, :]).then_inc(x0_in[p], 16)
                for odd in range(2):
                    sp.dma_start(x0_last[64 * odd:64 * odd + 64, p, :, :],
                                 mine[0, odd, FM:FM + 8, :].unsqueeze(1).broadcast_to(
                                     [8, J, HP * GB])).then_inc(x0_in[p], 16)

            load_x0(0, 0)
            load_x0(1, 1)
            sp.dma_start(w1z_sb[:, :, :], w1z.rearrange("(a p) n -> p a n", p=P)).then_inc(mlp_in, 16)
            sp.dma_start(w1d_sb[:, :], w1d).then_inc(mlp_in, 16)
            sp.dma_start(w2_sb[:, :, :], w2.rearrange("(a p) n -> p a n", p=P)).then_inc(mlp_in, 16)
            sp.dma_start(w3_sb[:, :], w3.rearrange("(a p) n -> p (a n)", p=P),
                         allow_slow_non_contiguous=True).then_inc(mlp_in, 16)
            sp.dma_start(dense_sb[:, :], dense_t).then_inc(mlp_in, 16)
            with sp.Fori(1, GROUPS // 2) as pair:
                for p in range(2):
                    load_x0(pair * 2 + p, p)
            sp.wait_ge(y_ready, GROUPS)
            sp.dma_start(y.rearrange("b a -> a b"), y_sb[:, :]).then_inc(stored, 16)
            sp.wait_ge(stored, 16)

        @block.gpsimd
        def _(pool):
            pool.dma_start(ids_sb[:, :, :], ids.rearrange("(t p) s -> p t s", p=P)).then_inc(ids_in, 16)
            pool.memset(ident[:, :], 0.0).then_inc(ident_done, 1)
            pool.wait_ge(ident_done, 1)
            pool.affine_select(out=ident[:, :], in_=ident[:, :], compare_op=ALU.not_equal, fill=1.0, base=0,
                               pattern=[[-1, P]], channel_multiplier=1).then_inc(ident_done, 1)
            pool.wait_ge(ids_in, 16)
            per_group = 16 * TPG * len(GATHERED)
            for g in range(GROUPS):
                if g >= 2:
                    pool.wait_ge(gathered[g % 2], per_group * (g // 2))
                for t in range(g * TPG, (g + 1) * TPG):
                    for s in GATHERED:
                        pool.indirect_dma_start(
                            out=e_all[:, t * E + s * D:t * E + (s + 1) * D], out_offset=None,
                            in_=tables[s], in_offset=bass.IndirectOffsetOnAxis(ap=ids_sb[:, t, s:s + 1], axis=0),
                        ).then_inc(gathered[g % 2], 16)

        @block.scalar
        def _(act):

            def stage_ids(n):
                act.dma_start(ids_i[:, n % 2, :], ids_t[n:n + 1, :].broadcast_to([RC, B])).then_inc(staged[n % 2], 16)

            stage_ids(0)
            stage_ids(1)
            act.dma_start(b2_sb[:, :], b2.rearrange("(a p) -> p a", p=P), allow_slow_non_contiguous=True).then_inc(mlp_in, 16)
            for n in range(len(ONE_HOT)):
                act.wait_ge(staged[n % 2], 16 * (n // 2 + 1))
                if n >= 2:
                    act.wait_ge(onehot_ready, CHUNK0[n - 1])
                act.activation(ids_h[:, n % 2, :], ids_i[:, n % 2, :], ACT.Copy).then_inc(ids_ready, 1)
                if n + 2 < len(ONE_HOT):
                    act.wait_ge(ids_ready, n + 1)
                    stage_ids(n + 2)

            def spread_group(g, p):
                if isinstance(g, int):
                    act.wait_ge(gathered[p], 16 * TPG * len(GATHERED) * (g // 2 + 1))
                else:
                    act.wait_ge(gathered[p], (g + (2 - p)) * (8 * TPG * len(GATHERED)))
                last = None
                for f0, count, i0, width in RUNS:
                    for odd in range(2):
                        src = window(g, i0, count, width)
                        if f0 < FM:
                            dst = spread[:, p, :, 0:MC * P].rearrange("p t (j h f) -> p t j h f", j=J, h=2)[
                                :, :, 0:width, odd, f0:f0 + 2 * count - 1:2]
                        else:
                            dst = spread[:, p, :, MC * P:EXW].rearrange("p t (h f j) -> p t h f j", h=2, f=8)[
                                :, :, odd, f0 - FM:f0 - FM + 2 * count - 1:2, 0:width].rearrange("p t f j -> p t j f")
                        last = act.activation(dst, src, ACT.Copy)
                last.then_inc(spread_ready, 1)

            def window(g, i0, count, width):
                first = e_all[:, bass.ds(g * (TPG * E) + i0, 1)]
                return bass.AP(first.tensor, first.offset, [list(first.ap[0]), [E, TPG], [1, width], [13, count]])

            def copy_xl(g, p):
                for i in range(XLP):
                    act.wait_ge(transposed, XLP * g + (i + 1))
                    n = min(2, NC - 2 * i)
                    act.activation(xl[:, p, 2 * i:2 * i + n, :],
                                   t_ps[(p + i) % 2][:, 0:n * GB].rearrange("p (a b) -> p a b", a=n),
                                   ACT.Copy).then_inc(xl_ready, 1)

            def relu1(m):
                for i in range(2):
                    act.wait_ge(h1_summed, 2 * m + (i + 1))
                    act.activation(h1_sb[:, 2 * i:2 * i + 2, :],
                                   h1_ps[i][:, :].rearrange("p (a b) -> p a b", a=2), ACT.Relu).then_inc(h1_ready, 1)

            def relu2(m):
                act.wait_ge(h2_summed, m + 1)
                for a in range(2):
                    act.activation(h2_sb[:, a, :], h2_ps[:, a * GB:(a + 1) * GB], ACT.Relu,
                                   bias=b2_sb[:, a:a + 1]).then_inc(h2_ready, 1)

            def copy_y(m):
                act.wait_ge(y_summed, m + 1)
                act.activation(y_sb[:, bass.ds(m * GB, GB)], y_ps[0:1, 0:GB], ACT.Copy).then_inc(y_ready, 1)

            def copy_z(g, p):
                act.wait_ge(contracted, NC * (g + 1))
                act.activation(z_sb[:, p, :, :], z_ps[p][:, :].rearrange("p (a b) -> p a b", a=2),
                               ACT.Copy).then_inc(z_ready, 1)

            act.wait_ge(looked_up, 2 * len(ONE_HOT))
            act.wait_ge(pads_done, 1)
            act.wait_ge(mlp_in, 16 * (MLP_LOADS))
            spread_group(0, 0)
            copy_xl(0, 0)
            spread_group(1, 1)

            def body(g, p):
                before = not isinstance(g, int) or g > 0
                if not isinstance(g, int) or g < GROUPS - 1:
                    copy_xl(g + 1, 1 - p)
                if before:
                    relu1(g - 1)
                if not isinstance(g, int) or g < GROUPS - 2:
                    spread_group(g + 2, p)
                if before:
                    relu2(g - 1)
                    copy_y(g - 1)
                copy_z(g, p)

            groups(act, body)
            relu1(GROUPS - 1)
            relu2(GROUPS - 1)
            copy_y(GROUPS - 1)

        @block.vector
        def _(dve):
            pads = spread[:, :, :, MC * P:EXW].rearrange("p a t (h c) -> p (a t) h c", h=2)
            dve.memset(pads[:, :, :, (F - FM) * J - 1:64], 0.0).then_inc(pads_done, 1)

            def split_tables():
                dve.wait_ge(table_in, 16)
                dve.tensor_copy(parts[:, :, 0, :], table_sb).then_inc(split_step, 1)
                dve.wait_ge(split_step, 1)
                dve.tensor_tensor(rest_sb, table_sb, parts[:, :, 0, :], ALU.subtract).then_inc(split_step, 1)
                dve.wait_ge(split_step, 2)
                dve.tensor_copy(parts[:, :, 1, :], rest_sb).then_inc(split_step, 1)
                dve.wait_ge(split_step, 3)
                dve.tensor_tensor(parts[:, :, 2, :], rest_sb, parts[:, :, 1, :], ALU.subtract).then_inc(split_step, 1)

            def spread_alpha():
                dve.wait_ge(prep_in, 16 * PREP_LOADS)
                dve.tensor_tensor(alpha_block, alpha_sb[:, :, :].unsqueeze(2).broadcast_to([P, F8, 8, K]),
                                  block_sb.unsqueeze(1).unsqueeze(3).broadcast_to([P, F8, 8, K]),
                                  ALU.mult).then_inc(alpha_spread, 1)

            def coef_operands():
                dve.wait_ge(coef_in, 16)
                dve.tensor_tensor(wh_sb[:, :, :], w_hv_sb[:, 0:K * H].rearrange("p (k h) -> p k h", k=K),
                                  w_hv_sb[:, K * H:].unsqueeze(2).broadcast_to([P, K, H]), ALU.mult).then_inc(wh_done, 1)
                dve.wait_ge(wh_done, 1)
                dve.tensor_tensor(wblock, wh_sb[:, :, :].unsqueeze(2).broadcast_to([P, K, J, H]),
                                  block_sb.unsqueeze(1).unsqueeze(3).broadcast_to([P, K, J, H]),
                                  ALU.mult).then_inc(lhs_done, 1)
                dve.wait_ge(bsum_done, 1)
                dve.tensor_copy(bsum_sb[:, 0:FM, :],
                                b_ps[0][:, :].rearrange("p (f k) -> p f k", k=K)).then_inc(bsum_copied, 1)
                dve.tensor_copy(bsum_sb[:, FM:FM + 8, :],
                                b_ps[1][:, 0:8 * K].rearrange("p (f k) -> p f k", k=K)).then_inc(bsum_copied, 1)
                dve.wait_ge(bsum_copied, 2)
                for h in range(2):
                    dve.tensor_tensor(
                        blast[:, :, h, :, :], bsum_sb[:, FM:FM + 8, :].rearrange("p f k -> p k f").unsqueeze(3).broadcast_to([P, K, 8, J]),
                        block_sb.unsqueeze(1).unsqueeze(2).broadcast_to([P, K, 8, J]), ALU.mult).then_inc(lhs_done, 1)

            def copy_coef():
                dve.wait_ge(c_done, 1)
                for h in range(2):
                    dve.tensor_scalar(
                        coef[:, 0:MC, :, h * K:(h + 1) * K].rearrange("p c a k -> p (c a) k"),
                        c_ps[:, :].rearrange("p (k c) -> p c k", k=K), half_sb[:, h:h + 1], None,
                        ALU.mult).then_inc(coef_done, 1)
                    dve.tensor_scalar(
                        coef[:, MC, :, h * K:(h + 1) * K],
                        c4_ps[:, 0:K * H].rearrange("p (k a h) -> p h a k", k=K, h=2)[:, h], half_sb[:, 2 + h:3 + h], None,
                        ALU.mult).then_inc(coef_done, 1)

            def make_onehot(n, c):
                at = CHUNK0[n] + c
                if at >= SLOTS:
                    dve.wait_ge(onehot_used, at - SLOTS + 1)
                dve.tensor_scalar(onehot[:, at % SLOTS, :], ids_h[:, n % 2, :], row_sb[:, at:at + 1], None,
                                  ALU.is_equal).then_inc(onehot_ready, 1)

            def take_rows(n):
                dve.wait_ge(onehot_used, CHUNK0[n] + CHUNKS[n])
                s = ONE_HOT[n]
                for a in range(2):
                    dve.tensor_reduce(
                        e_all[:, :].rearrange("p (t i) -> p t i", i=E)[:, 8 * a:8 * a + 8, s * D:(s + 1) * D],
                        look_ps[n % 2][a][:, 0:8 * PARTS * D].rearrange("p (t c d) -> p t d c", t=8, c=PARTS),
                        AX_X, ALU.add).then_inc(looked_up, 1)

            dve.wait_ge(masks_in, 16)
            for n in range(len(ONE_HOT)):
                dve.wait_ge(ids_ready, n + 1)
                for c in range(CHUNKS[n]):
                    make_onehot(n, c)
                    if n == 0 and c == SLOTS - 1:
                        split_tables()
                    if n > 0 and c == SLOTS:
                        take_rows(n - 1)
                if n == 0:
                    spread_alpha()
                if n == 1:
                    coef_operands()
                if n == 2:
                    copy_coef()
            take_rows(len(ONE_HOT) - 1)

            def body(g, p):
                if isinstance(g, int):
                    dve.wait_ge(x0_in[p], 16 * X0_LOADS * (g // 2 + 1))
                else:
                    dve.wait_ge(x0_in[p], (g + (2 - p)) * (8 * X0_LOADS))
                for c in range(NC):
                    dve.wait_ge(xl_ready, XLP * g + (c // 2 + 1))
                    if not isinstance(g, int) or g > 0:
                        dve.wait_ge(contracted, NC * (g - 1) + (c + 1))
                    x0 = x0_main if c < MC else x0_last
                    dve.tensor_tensor(prod[:, c, :, :], x0[:, p, :, :],
                                      xl[:, p, c, :].unsqueeze(1).broadcast_to([P, HP, GB]),
                                      ALU.mult).then_inc(product_ready, 1)

            groups(dve, body)

        @block.tensor
        def _(pe):
            def sum_alpha():
                pe.wait_ge(prep_in, 16 * PREP_LOADS)
                pe.wait_ge(alpha_spread, 1)
                for c in range(F8):
                    last = pe.matmul(b_ps[c // 4][:, c % 4 * P:(c % 4 + 1) * P], mask_sb[:, c * P:(c + 1) * P],
                                     alpha_block[:, c, :, :].rearrange("p f k -> p (f k)"), start=True, stop=True)
                last.then_inc(bsum_done, 1)

            def make_coef():
                pe.wait_ge(bsum_copied, 2)
                pe.wait_ge(lhs_done, 3)
                for k in range(K):
                    for j in range(2):
                        for odd in range(2):
                            row = 64 * j + 32 * odd
                            pe.matmul(c_ps[row:row + FM, k * MC * HP:(k + 1) * MC * HP], bsum_sb[:, 0:FM, k],
                                      wblock[:, k, j::2, odd::2], start=True, stop=True)
                for k in range(K):
                    last = pe.matmul(c4_ps[:, k * H:(k + 1) * H], blast[:, k, :, :, :].rearrange("p h f j -> p (h f j)"),
                                     wh_sb[:, k, :], start=True, stop=True)
                last.then_inc(c_done, 1)

            def look_up(n, c):
                at = CHUNK0[n] + c
                if c == 0 and n >= 2:
                    pe.wait_ge(looked_up, 2 * (n - 1))
                pe.wait_ge(onehot_ready, at + 1)
                for t in range(TILES):
                    last = pe.matmul(look_ps[n % 2][t // 8][:, t % 8 * PARTS * D:(t % 8 + 1) * PARTS * D],
                                     onehot[:, at % SLOTS, t * P:(t + 1) * P],
                                     parts[:, at, :, :].rearrange("p c d -> p (c d)"),
                                     start=(c == 0 and t % 8 == 0), stop=(c == CHUNKS[n] - 1),
                                     skip_group_check=True)
                last.then_inc(onehot_used, 1)

            pe.wait_ge(split_step, 4)
            for n in range(len(ONE_HOT)):
                for c in range(CHUNKS[n]):
                    look_up(n, c)
                if n == 0:
                    sum_alpha()
                if n == 1:
                    make_coef()

            def transpose_values(g, p):
                pe.wait_ge(spread_ready, g + 1)
                for i in range(XLP):
                    if not isinstance(g, int) or g > 0 or i >= 2:
                        pe.wait_ge(xl_ready, XLP * g + (i - 1))
                    for c in range(2 * i, min(2 * i + 2, NC)):
                        for t in range(TPG):
                            col = c % 2 * GB + t * P
                            last = pe.transpose(t_ps[(p + i) % 2][:, col:col + P],
                                                spread[:, p, t, c * P:(c + 1) * P], ident[:, :])
                    last.then_inc(transposed, 1)

            def contract(g, p, c):
                pe.wait_ge(product_ready, NC * g + (c + 1))
                for a in range(2):
                    for q in range(4):
                        last = pe.matmul(z_ps[p][32 * q:32 * q + 32, a * GB:(a + 1) * GB], coef[:, c, 4 * a + q, :],
                                         prod[:, c, 4 * a + q, :], start=(c == 0 and a == 0), stop=(c == NC - 1),
                                         skip_group_check=True)
                last.then_inc(contracted, 1)

            def layer1(m, p, i):
                for a in range(2):
                    out = h1_ps[i][:, a * GB:(a + 1) * GB]
                    cols = slice((2 * i + a) * P, (2 * i + a + 1) * P)
                    pe.matmul(out, w1d_sb[:, cols], dense_cols(m), start=True, stop=False)
                    pe.matmul(out, w1z_sb[:, 0, cols], z_sb[:, p, 0, :], start=False, stop=False)
                    last = pe.matmul(out, w1z_sb[:, 1, cols], z_sb[:, p, 1, :], start=False, stop=True)
                last.then_inc(h1_summed, 1)

            def dense_cols(m):
                return dense_sb[:, bass.ds(m * GB, GB)]

            def layer2(m):
                pe.wait_ge(h1_ready, 2 * m + 2)
                for a in range(2):
                    for c in range(N1 // P):
                        last = pe.matmul(h2_ps[:, a * GB:(a + 1) * GB], w2_sb[:, c, a * P:(a + 1) * P],
                                         h1_sb[:, c, :], start=(c == 0), stop=(c == N1 // P - 1))
                last.then_inc(h2_summed, 1)

            def layer3(m):
                pe.wait_ge(h2_ready, 2 * m + 2)
                for a in range(2):
                    last = pe.matmul(y_ps[0:1, 0:GB], w3_sb[:, a:a + 1], h2_sb[:, a, :], start=(a == 0), stop=(a == 1))
                last.then_inc(y_summed, 1)

            pe.wait_ge(ident_done, 2)
            pe.wait_ge(coef_done, 4)
            pe.wait_ge(mlp_in, 16 * (MLP_LOADS))
            pe.wait_ge(looked_up, 2 * len(ONE_HOT))

            def body(g, p):
                before = not isinstance(g, int) or g > 0
                after = not isinstance(g, int) or g < GROUPS - 1
                if after:
                    transpose_values(g + 1, 1 - p)
                contract(g, p, 0)
                if before:
                    pe.wait_ge(z_ready, g)
                    layer1(g - 1, 1 - p, 0)
                contract(g, p, 1)
                if before:
                    layer1(g - 1, 1 - p, 1)
                contract(g, p, 2)
                contract(g, p, 3)
                if before:
                    layer2(g - 1)
                contract(g, p, 4)
                if before:
                    layer3(g - 1)

            transpose_values(0, 0)
            groups(pe, body)
            pe.wait_ge(z_ready, GROUPS)
            m, p = GROUPS - 1, (GROUPS - 1) % 2
            layer1(m, p, 0)
            layer1(m, p, 1)
            layer2(m)
            layer3(m)


def kernel(dense_ctx, ids, r_x0, W_top1, b_top1, W_top2, b_top2, W_top3, L0_rec_w, L0_rec_alpha, L0_rec_hv, **tables):
    import numpy as _np
    import concourse.bacc as _bacc
    from concourse import mybir as _mybir
    from concourse.bass_utils import run_bass_kernel_spmd as _run

    flat = lambda a: _np.ascontiguousarray(_np.asarray(a))
    ids, w1, hv = flat(ids), flat(W_top1), flat(L0_rec_hv)
    slot_mask, masks = shape_constants()
    x0 = _np.zeros((B, FM + 8, H), _np.float32)
    x0[:, 0:F] = flat(r_x0)
    arrays = {
        "ids": ids,
        "ids_t": flat(ids[:, ONE_HOT].T),
        **{f"tbl_{s}": flat(tables[f"tbl_{s}"]) for s in GATHERED},
        "x0_g": flat(x0.reshape(GROUPS, GB, FM + 8, HP, 2).transpose(0, 4, 2, 3, 1).reshape(GROUPS, 2, FM + 8, HP * GB)),
        "small_tables": _np.concatenate([flat(tables[f"tbl_{s}"]).reshape(RC, -1) for s in ONE_HOT], 1),
        "dense_t": _np.concatenate([flat(dense_ctx).T, _np.ones((1, B), _np.float32)], 0),
        "alpha": _np.concatenate([flat(L0_rec_alpha), _np.zeros(((8 * F8 - F) * S, K), _np.float32)], 0),
        "w_hv": _np.concatenate([flat(L0_rec_w).transpose(2, 0, 1).reshape(D, K * H), hv[:, :, 0].T], 1),
        "w1z": flat(w1[:K * H].reshape(K, H, N1).transpose(1, 0, 2).reshape(K * H, N1)),
        "w1d": _np.concatenate([w1[K * H:], flat(b_top1)[None]], 0),
        "w2": flat(W_top2),
        "b2": flat(b_top2),
        "w3": flat(W_top3),
        "slot_mask": slot_mask,
        "masks": masks,
    }
    nc = _bacc.Bacc("TRN2", target_bir_lowering=False, num_devices=1)
    aps = {n: nc.dram_tensor(n, a.shape, _mybir.dt.from_np(a.dtype), kind="ExternalInput").ap() for n, a in arrays.items()}
    table_aps = {s: aps.pop(f"tbl_{s}") for s in GATHERED}
    y = nc.dram_tensor("y", (B, 1), _mybir.dt.float32, kind="ExternalOutput").ap()
    dlrm_tower(nc, tables=table_aps, y=y, **aps)
    return _run(nc, [arrays], core_ids=[0]).results[0]["y"]
```

```python
from contextlib import ExitStack

import numpy as np

import concourse.bass as bass
from concourse import mybir

F32 = mybir.dt.float32
F32R = mybir.dt.float32r
F16 = mybir.dt.float16
BF16 = mybir.dt.bfloat16
I32 = mybir.dt.int32
ALU = mybir.AluOpType
ACT = mybir.ActivationFunctionType
AX_X = mybir.AxisListType.X

P = 128
VOCAB = [12500, 1250, 1000, 1250, 12500, 125000, 125000, 125000, 1250, 1000, 12500, 1000, 1250, 12500, 1250, 1250]
B, F, H, D, K = 2048, 39, 16, 16, 16
S = len(VOCAB)
E = S * D
REP = F
BLOCK = S * D
J = 8
ONE_HOT = [2, 9, 11, 1, 3, 8, 12]
GATHERED = [s for s in range(S) if s not in ONE_HOT]
RC = 125
CHUNKS = [VOCAB[s] // RC for s in ONE_HOT]
CHUNK0 = [sum(CHUNKS[:n]) for n in range(len(ONE_HOT))]
NCHUNK = sum(CHUNKS)
PARTS = 3
TILES = B // P
HALF = B // 2
HT = HALF // P
GB = 256
TPG = GB // P
SLOTS = 8
GROUPS = B // GB
STAGES = 3
HP = H // 2
F8 = -(-F // 8)
FM = 32
MC = J // 2
NC = MC + 1
EXW = MC * P + P
XLP = (NC + 1) // 2
N1, N2 = 512, 256
DC = 16


def first_value(f):
    return BLOCK * f // REP


def spread_runs():
    runs = []
    for lo, hi in ((0, FM), (FM, F)):
        for odd in (0, 1):
            fs = list(range(lo + odd, hi, 2))
            while fs:
                n = 1
                while n < len(fs) and first_value(fs[n]) == first_value(fs[0]) + 13 * n:
                    n += 1
                n -= n > 1 and first_value(fs[n - 1]) + J > E
                width = min(J, E - first_value(fs[0]))
                runs.append((fs[0], n, first_value(fs[0]), width))
                fs = fs[n:]
    return runs


RUNS = spread_runs()
NSMALL = len(ONE_HOT)
LOOKUPS = [(n, c) for n in range(NSMALL) for c in range(CHUNKS[n])]

FIRST_TABLES = CHUNK0[3]
SPLIT_AT, MULTIPLY_AT, SUM_AT = 3, 3, 7
COEF_AT, COEF_EVERY = 26, 2
DENSE_AT = 45
TAKE_AT = 5
WEIGHTS_AFTER, SUMS_AFTER = 3, 5
LATE_FIRST = 22
LATE_STEPS = 12
LAYER1_AT, LAYER2_AT = (0, 1), 3
TRANSPOSES_AT = 3
Z_LOW_AT, H1_LOW_AT = 1, (2, 3)
SPLIT_FROM = 2
ROUND_AT = 2


def late_lookups(step):
    if step < 0:
        return range(LATE_FIRST)
    if step >= LATE_STEPS:
        return range(0)
    return range(LATE_FIRST + (NCHUNK - LATE_FIRST) * step // LATE_STEPS,
                 LATE_FIRST + (NCHUNK - LATE_FIRST) * (step + 1) // LATE_STEPS)


def gathered_by(g):
    return 16 * TPG * len(GATHERED) * (g // 2 + 1)


def shape_constants():
    e = np.arange(F * BLOCK).reshape(F, D, D)
    first = np.array([first_value(f) for f in range(F)])[:, None, None, None]
    slot = (e[:, :, None, :] // REP) == first + np.arange(J)[None, None, :, None]
    slot_mask = np.zeros((F8 * 8, D, P), np.float32)
    slot_mask[0:F] = slot.reshape(F, D, P)
    slot_mask = slot_mask.reshape(F8, P, P).transpose(1, 0, 2).reshape(P, F8 * P)
    slot_block = (np.arange(P)[:, None] // D == np.arange(J)[None]).astype(np.float32)
    rows = np.arange(P)
    half = np.stack([rows // FM % 2 == 0, rows // FM % 2 == 1, rows // 64 == 0, rows // 64 == 1], 1)
    table_row = np.concatenate([np.arange(P)[:, None] * c + np.arange(c) for c in CHUNKS], 1)
    return slot_mask, np.concatenate([slot_block, half, table_row], 1).astype(np.float32)


def dlrm_tower(nc, ids, ids_t, small_tables, tables, x0_g, dense_t, alpha, w_hv, w1z, w1d, w2, b2, w3,
               slot_mask, masks, y):
    with ExitStack() as ctx:
        def sb(name, shape, dt=F32):
            return ctx.enter_context(nc.sbuf_tensor(name, shape, dt))

        def sem(name):
            return ctx.enter_context(nc.semaphore(name))

        ident = sb("ident", [P, P])
        warm = sb("warm", [P, 2])
        ids_sb = sb("ids_sb", [P, TILES, S], I32)
        e_all = sb("e_all", [P, TILES * E])
        spread = sb("spread", [P, 2, TPG, EXW])
        xl = sb("xl", [P, 2, NC, GB])
        x0_main = sb("x0_main", [P, 2, HP, GB])
        x0_last = sb("x0_last", [P, 2, HP, GB])
        prod = sb("prod", [P, NC, HP, GB])
        coef = sb("coef", [P, NC, HP, 2 * K])
        z_sb = sb("z_sb", [P, 2, 2, GB])
        h1_sb = sb("h1_sb", [P, N1 // P, GB])
        h2_sb = sb("h2_sb", [P, N2 // P, GB])
        y_sb = sb("y_sb", [P, GROUPS, GB // 4])
        dense_sb = sb("dense_sb", [P, B], F32R)
        w1z_sb = sb("w1z_sb", [P, 2, N1])
        w1d_sb = sb("w1d_sb", [P, N1], F32R)
        w2_sb = sb("w2_sb", [P, N1 // P, N2])
        b2_sb = sb("b2_sb", [P, N2 // P])
        w3_sb = sb("w3_sb", [P, N2 // P])
        masks_sb = sb("masks_sb", [P, J + 4 + NCHUNK])
        block_sb, half_sb, row_sb = masks_sb[:, 0:J], masks_sb[:, J:J + 4], masks_sb[0:RC, J + 4:J + 4 + NCHUNK]
        parts = sb("parts", [RC, NCHUNK, PARTS, D], BF16)
        onehot = sb("onehot", [RC, SLOTS, HALF], BF16)
        alpha_sb = sb("alpha_sb", [P, F8, K])
        w_hv_sb = sb("w_hv_sb", [P, K * H + K])
        wh_sb = sb("wh_sb", [P, K, H])
        bsum_sb = sb("bsum_sb", [P, F + 1, K])
        arena = prod[:, :, :, :].rearrange("p c h b -> p (c h b)")
        at = [0]

        def early(n):
            at[0] += n
            assert at[0] <= NC * HP * GB
            return arena[:, at[0] - n:at[0]]

        mask_sb = early(F8 * P)
        alpha_block = early(F8 * 8 * K).rearrange("p (c f k) -> p c f k", c=F8, f=8)
        wblock = early(K * J * H).rearrange("p (k j h) -> p k j h", k=K, j=J)
        blast = early(K * 2 * 8 * J).rearrange("p (k h f j) -> p k h f j", k=K, h=2, j=J)
        table_sb = early(NCHUNK * D)[0:RC, :].rearrange("p (c d) -> p c d", d=D)
        rest_sb = early((NCHUNK - FIRST_TABLES) * D)[0:RC, :].rearrange("p (c d) -> p c d", d=D)

        ids_i = early(STAGES * HALF)[0:RC, :].bitcast(I32).rearrange("p (a b) -> p a b", a=STAGES)
        dense_f = [spread[:, a, :, :].rearrange("p t c -> p (t c)")[:, 0:HALF] for a in range(2)]
        w1d_f = z_sb[:, 0, :, :].rearrange("p a b -> p (a b)")

        with nc.sbuf_tensor("ids_h", [RC, NSMALL, B], F16) as ids_h:
            pass
        splits = sb("splits", [P, NSMALL * B // 2], F32R)
        w1z_parts = splits[:, 0:4 * N1].rearrange("p (i a n) -> p i a n", i=2, a=2)
        w2_parts = splits[:, 4 * N1:8 * N1].rearrange("p (i a n) -> p i a n", i=2, a=N1 // P)
        z_high, z_low = [splits[:, n * N1:(n + 1) * N1].rearrange("p (a b) -> p a b", a=2) for n in (8, 9)]
        h1_high, h1_low = [splits[:, n * N1:(n + 2) * N1].rearrange("p (a b) -> p a b", a=N1 // P) for n in (10, 12)]

        bank = [ctx.enter_context(nc.psum_tensor(f"bank{i}", [P, 512], F32)) for i in range(8)]
        z_ps = bank[0:2]
        t_ps = bank[2:4]
        h1_ps = bank[4:6]
        look_ps = bank[6:8]

        def h2_ps(m):
            return h1_ps[1] if m < SPLIT_FROM else look_ps[0]

        def y_ps(m):
            return h1_ps[0] if m < SPLIT_FROM else look_ps[1]

        b_ps, c_ps, c4_ps = bank[0:2], bank[4], bank[5]

        prep_in = sem("prep_in")
        masks_in = sem("masks_in")
        coef_in = sem("coef_in")
        table_in = sem("table_in")
        mlp_in = sem("mlp_in")
        pads_done = sem("pads_done")
        dense_in = sem("dense_in")
        dense_zeroed = sem("dense_zeroed")
        dense_high = sem("dense_high")
        dense_low = sem("dense_low")
        warm_ready = sem("warm_ready")
        ident_done = sem("ident_done")
        ids_in = sem("ids_in")
        staged = [sem(f"staged{i}") for i in range(STAGES)]
        ids_ready = sem("ids_ready")
        wh_done = sem("wh_done")
        alpha_spread = sem("alpha_spread")
        bsum_done = sem("bsum_done")
        bsum_copied = sem("bsum_copied")
        wblock_done = sem("wblock_done")
        blast_done = sem("blast_done")
        c_done = sem("c_done")
        coef_done = sem("coef_done")
        split_step = sem("split_step")
        onehot_ready = sem("onehot_ready")
        onehot_used = sem("onehot_used")
        looked_up = sem("looked_up")
        gathered = [sem(f"gathered{i}") for i in range(2)]
        x0_in = [sem(f"x0_in{i}") for i in range(2)]
        spread_ready = sem("spread_ready")
        transposed = sem("transposed")
        xl_ready = sem("xl_ready")
        product_ready = sem("product_ready")
        contracted = sem("contracted")
        z_ready = sem("z_ready")
        weights_high = sem("weights_high")
        weights_low = sem("weights_low")
        z_low_ready = sem("z_low_ready")
        h1_summed = sem("h1_summed")
        h1_ready = sem("h1_ready")
        h1_low_ready = sem("h1_low_ready")
        h2_summed = sem("h2_summed")
        h2_ready = sem("h2_ready")
        y_summed = sem("y_summed")
        y_ready = sem("y_ready")
        stored = sem("stored")

        PREP_LOADS, MLP_LOADS, X0_LOADS, DENSE_LOADS = 2, 4, 4, 12

        block = ctx.enter_context(nc.Block())

        @block.sync
        def _(sp):
            sp.dma_start(table_sb, small_tables.rearrange("p (c d) -> p c d", d=D)).then_inc(table_in, 16)
            sp.dma_start(masks_sb[:, :], masks).then_inc(masks_in, 16)
            sp.dma_start(alpha_sb[:, :, :], alpha.rearrange("(c p) k -> p c k", p=P)).then_inc(prep_in, 16)
            sp.dma_start(mask_sb, slot_mask).then_inc(prep_in, 16)
            sp.dma_start(w_hv_sb[:, :], w_hv.unsqueeze(0).broadcast_to([J, D, K * H + K])).then_inc(coef_in, 16)
            sp.wait_ge(dense_zeroed, 3)
            for q in range(4):
                rows = slice(32 * q, 32 * q + DC + 1)
                for a in range(2):
                    sp.dma_start(dense_f[a][rows, :], dense_t[:, a * HALF:(a + 1) * HALF]).then_inc(dense_in, 16)
                sp.dma_start(w1d_f[rows, :], w1d).then_inc(dense_in, 16)

            def load_x0(g, p):
                if g >= 2:
                    sp.wait_ge(product_ready, NC * (g - 1))
                mine = x0_g[g:g + 1]
                for j in range(2):
                    sp.dma_start(x0_main[64 * j:64 * j + 2 * FM, p, :, :],
                                 mine[0, :, 0:FM, :]).then_inc(x0_in[p], 16)
                for odd in range(2):
                    sp.dma_start(x0_last[64 * odd:64 * odd + 64, p, :, :],
                                 mine[0, odd, FM:FM + 8, :].unsqueeze(1).broadcast_to(
                                     [8, J, HP * GB])).then_inc(x0_in[p], 16)

            load_x0(0, 0)
            load_x0(1, 1)
            sp.dma_start(w1z_sb[:, :, :], w1z.rearrange("(a p) n -> p a n", p=P)).then_inc(mlp_in, 16)
            sp.dma_start(w2_sb[:, :, :], w2.rearrange("(a p) n -> p a n", p=P)).then_inc(mlp_in, 16)
            sp.dma_start(w3_sb[:, :], w3.rearrange("(a p) n -> p (a n)", p=P),
                         allow_slow_non_contiguous=True).then_inc(mlp_in, 16)
            for g in range(2, GROUPS):
                load_x0(g, g % 2)
            sp.wait_ge(y_ready, GROUPS)
            sp.dma_start(y.rearrange("(g q b) a -> q g (b a)", g=GROUPS, q=4), y_sb[0:97:32, :, :]).then_inc(stored, 16)
            sp.wait_ge(stored, 16)

        @block.gpsimd
        def _(pool):
            pool.dma_start(ids_sb[:, :, :], ids.rearrange("(t p) s -> p t s", p=P)).then_inc(ids_in, 16)
            pool.memset(ident[:, :], 0.0).then_inc(ident_done, 1)
            pool.wait_ge(ident_done, 1)
            pool.affine_select(out=ident[:, :], in_=ident[:, :], compare_op=ALU.not_equal, fill=1.0, base=0,
                               pattern=[[-1, P]], channel_multiplier=1).then_inc(ident_done, 1)
            pool.wait_ge(ids_in, 16)
            for g in range(GROUPS):
                if g >= 2:
                    pool.wait_ge(gathered[g % 2], gathered_by(g - 2))
                for t in range(g * TPG, (g + 1) * TPG):
                    for s in GATHERED:
                        pool.indirect_dma_start(
                            out=e_all[:, t * E + s * D:t * E + (s + 1) * D], out_offset=None,
                            in_=tables[s], in_offset=bass.IndirectOffsetOnAxis(ap=ids_sb[:, t, s:s + 1], axis=0),
                        ).then_inc(gathered[g % 2], 16)

        @block.scalar
        def _(act):

            def stage_ids(i):
                n, a = i % NSMALL, i // NSMALL
                act.dma_start(ids_i[:, i % STAGES, :], ids_t[n:n + 1, a * HALF:(a + 1) * HALF].broadcast_to(
                    [RC, HALF])).then_inc(staged[i % STAGES], 16)

            def cast_ids(i):
                n, a = i % NSMALL, i // NSMALL
                act.wait_ge(staged[i % STAGES], 16 * (i // STAGES + 1))
                act.activation(ids_h[:, n, a * HALF:(a + 1) * HALF], ids_i[:, i % STAGES, :], ACT.Copy).then_inc(ids_ready, 1)
                if i + STAGES < 2 * NSMALL:
                    act.wait_ge(ids_ready, i + 1)
                    stage_ids(i + STAGES)

            for i in range(STAGES):
                stage_ids(i)
            act.wait_ge(warm_ready, 1)
            act.activation(warm[:, 1:2], warm[:, 0:1], ACT.Copy)
            act.dma_start(b2_sb[:, :], b2.rearrange("(a p) -> p a", p=P), allow_slow_non_contiguous=True).then_inc(mlp_in, 16)
            def spread_weights():
                act.wait_ge(wh_done, 1)
                act.wait_ge(masks_in, 16)
                for j in range(J):
                    last = act.activation(wblock[:, :, j, :], wh_sb[:, :, :], ACT.Copy, scale=block_sb[:, j:j + 1])
                last.then_inc(wblock_done, 1)

            def spread_sums():
                act.wait_ge(bsum_done, 1)
                act.activation(bsum_sb[:, FM:FM + 8, :], b_ps[1][:, 0:8 * K].rearrange("p (f k) -> p f k", k=K),
                               ACT.Copy).then_inc(bsum_copied, 1)
                act.activation(bsum_sb[:, 0:FM, :], b_ps[0][:, :].rearrange("p (f k) -> p f k", k=K),
                               ACT.Copy).then_inc(bsum_copied, 1)
                act.wait_ge(bsum_copied, 1)
                for j in range(J):
                    last = act.activation(
                        blast[:, :, :, :, j],
                        bsum_sb[:, FM:FM + 8, :].rearrange("p f k -> p k f").unsqueeze(2).broadcast_to([P, K, 2, 8]),
                        ACT.Copy, scale=block_sb[:, j:j + 1])
                last.then_inc(blast_done, 1)

            def copy_coef():
                act.wait_ge(c_done, 1)
                for h in range(2):
                    act.activation(coef[:, 0:MC, :, h * K:(h + 1) * K].rearrange("p c a k -> p (c a) k"),
                                   c_ps[:, :].rearrange("p (k c) -> p c k", k=K), ACT.Copy, scale=half_sb[:, h:h + 1])
                    last = act.activation(coef[:, MC, :, h * K:(h + 1) * K],
                                          c4_ps[:, 0:K * H].rearrange("p (k a h) -> p h a k", k=K, h=2)[:, h],
                                          ACT.Copy, scale=half_sb[:, 2 + h:3 + h])
                last.then_inc(coef_done, 1)

            for i in range(NSMALL):
                cast_ids(i)
                if i == WEIGHTS_AFTER:
                    spread_weights()
                if i == SUMS_AFTER:
                    spread_sums()
            act.wait_ge(dense_in, 16 * DENSE_LOADS)
            for a in range(2):
                act.activation(dense_sb[:, a * HALF:(a + 1) * HALF], dense_f[a], ACT.Copy).then_inc(dense_high, 1)
            act.activation(w1d_sb[:, :], w1d_f, ACT.Copy).then_inc(dense_high, 1)
            for i in range(NSMALL, 2 * NSMALL):
                cast_ids(i)

            def spread_group(g, p):
                act.wait_ge(gathered[p], gathered_by(g))
                act.wait_ge(looked_up, NSMALL if g < GROUPS // 2 else 2 * NSMALL)
                last = None
                for f0, count, i0, width in RUNS:
                    for odd in range(2):
                        src = window(g, i0, count, width)
                        if f0 < FM:
                            dst = spread[:, p, :, 0:MC * P].rearrange("p t (j h f) -> p t j h f", j=J, h=2)[
                                :, :, 0:width, odd, f0:f0 + 2 * count - 1:2]
                        else:
                            dst = spread[:, p, :, MC * P:EXW].rearrange("p t (h f j) -> p t h f j", h=2, f=8)[
                                :, :, odd, f0 - FM:f0 - FM + 2 * count - 1:2, 0:width].rearrange("p t f j -> p t j f")
                        last = act.activation(dst, src, ACT.Copy)
                last.then_inc(spread_ready, 1)

            def window(g, i0, count, width):
                first = e_all[:, g * TPG * E + i0:g * TPG * E + i0 + 1]
                return bass.AP(first.tensor, first.offset, [list(first.ap[0]), [E, TPG], [1, width], [13, count]])

            def copy_xl(g, p):
                for i in range(XLP):
                    act.wait_ge(transposed, XLP * g + (i + 1))
                    n = min(2, NC - 2 * i)
                    act.activation(xl[:, p, 2 * i:2 * i + n, :],
                                   t_ps[(p + i) % 2][:, 0:n * GB].rearrange("p (a b) -> p a b", a=n),
                                   ACT.Copy).then_inc(xl_ready, 1)

            def relu1(m, i):
                act.wait_ge(h1_summed, 2 * m + (i + 1))
                out = h1_sb[:, :, :] if m < SPLIT_FROM else h1_high
                act.activation(out[:, 2 * i:2 * i + 2, :],
                               h1_ps[i][:, :].rearrange("p (a b) -> p a b", a=2), ACT.Relu).then_inc(h1_ready, 1)

            def relu2(m):
                act.wait_ge(h2_summed, m + 1)
                for a in range(2):
                    act.activation(h2_sb[:, a, :], h2_ps(m)[:, a * GB:(a + 1) * GB], ACT.Relu,
                                   bias=b2_sb[:, a:a + 1]).then_inc(h2_ready, 1)

            def copy_y(m):
                act.wait_ge(y_summed, m + 1)
                act.activation(y_sb[:, m, :], y_ps(m)[:, 0:GB // 4], ACT.Copy).then_inc(y_ready, 1)

            def copy_z(g, p):
                act.wait_ge(contracted, NC * (g + 1))
                out = z_sb[:, p, :, :] if g < SPLIT_FROM else z_high
                act.activation(out, z_ps[p][:, :].rearrange("p (a b) -> p a b", a=2),
                               ACT.Copy).then_inc(z_ready, 1)

            def round_weights():
                act.wait_ge(onehot_ready, 2 * NCHUNK)
                act.activation(w1z_parts[:, 0, :, :], w1z_sb[:, :, :], ACT.Copy).then_inc(weights_high, 1)
                act.activation(w2_parts[:, 0, :, :], w2_sb[:, :, :], ACT.Copy).then_inc(weights_high, 1)

            act.wait_ge(pads_done, 1)
            act.wait_ge(mlp_in, 16 * MLP_LOADS)
            spread_group(0, 0)
            copy_coef()
            copy_xl(0, 0)
            spread_group(1, 1)
            for g in range(GROUPS):
                p = g % 2
                for c in range(NC):
                    if g < GROUPS - 1 and c == TRANSPOSES_AT:
                        copy_xl(g + 1, 1 - p)
                    for i in range(2):
                        if g > 0 and c == LAYER1_AT[i]:
                            relu1(g - 1, i)
                    if g == SPLIT_FROM and c == ROUND_AT:
                        round_weights()
                if g > 0:
                    relu2(g - 1)
                    copy_y(g - 1)
                copy_z(g, p)
                if g < GROUPS - 2:
                    spread_group(g + 2, p)
            for i in range(2):
                relu1(GROUPS - 1, i)
            relu2(GROUPS - 1)
            copy_y(GROUPS - 1)

        @block.vector
        def _(dve):
            dve.memset(warm[:, 0:1], 0.0).then_inc(warm_ready, 1)
            for a in range(2):
                dve.memset(dense_f[a], 0.0).then_inc(dense_zeroed, 1)
            dve.memset(w1d_f, 0.0).then_inc(dense_zeroed, 1)

            def split_dense():
                dve.wait_ge(dense_high, 3)
                for a in range(2):
                    cols = slice(a * HALF, (a + 1) * HALF)
                    dve.tensor_tensor(dense_sb[64:P, cols], dense_f[a][64:P, :], dense_sb[64:P, cols],
                                      ALU.subtract).then_inc(dense_low, 1)
                for q in (32, 96):
                    dve.tensor_tensor(w1d_sb[q:q + 32, :], w1d_f[q:q + 32, :], w1d_sb[q:q + 32, :],
                                      ALU.subtract).then_inc(dense_low, 1)
                dve.wait_ge(dense_low, 4)
                pads = spread[:, :, :, MC * P:EXW].rearrange("p a t (h c) -> p (a t) h c", h=2)
                dve.memset(pads[:, :, :, (F - FM) * J - 1:64], 0.0).then_inc(pads_done, 1)

            def split_tables(part, chunks):
                rows = table_sb[:, chunks, :]
                rest = rest_sb[:, 0:chunks.stop - chunks.start, :]
                dve.tensor_copy(parts[:, chunks, 0, :], rows).then_inc(split_step, 1)
                dve.wait_ge(split_step, 4 * part + 1)
                dve.tensor_tensor(rest, rows, parts[:, chunks, 0, :], ALU.subtract).then_inc(split_step, 1)
                dve.wait_ge(split_step, 4 * part + 2)
                dve.tensor_copy(parts[:, chunks, 1, :], rest).then_inc(split_step, 1)
                dve.wait_ge(split_step, 4 * part + 3)
                dve.tensor_tensor(parts[:, chunks, 2, :], rest, parts[:, chunks, 1, :], ALU.subtract).then_inc(split_step, 1)

            def spread_alpha():
                dve.wait_ge(prep_in, 16 * PREP_LOADS)
                dve.tensor_tensor(alpha_block, alpha_sb[:, :, :].unsqueeze(2).broadcast_to([P, F8, 8, K]),
                                  block_sb.unsqueeze(1).unsqueeze(3).broadcast_to([P, F8, 8, K]),
                                  ALU.mult).then_inc(alpha_spread, 1)

            def multiply_weights():
                dve.wait_ge(coef_in, 16)
                dve.tensor_tensor(wh_sb[:, :, :], w_hv_sb[:, 0:K * H].rearrange("p (k h) -> p k h", k=K),
                                  w_hv_sb[:, K * H:].unsqueeze(2).broadcast_to([P, K, H]), ALU.mult).then_inc(wh_done, 1)

            def make_onehot(a, i):
                n, c = LOOKUPS[i]
                at = a * NCHUNK + i
                if at >= SLOTS:
                    dve.wait_ge(onehot_used, at - SLOTS + 1)
                if c == 0:
                    dve.wait_ge(ids_ready, a * NSMALL + n + 1)
                dve.tensor_scalar(onehot[:, at % SLOTS, :], ids_h[:, n, a * HALF:(a + 1) * HALF],
                                  row_sb[:, i:i + 1], None, ALU.is_equal).then_inc(onehot_ready, 1)

            def take_rows(a, n):
                dve.wait_ge(onehot_used, a * NCHUNK + CHUNK0[n] + CHUNKS[n])
                s = ONE_HOT[n]
                dve.tensor_reduce(
                    e_all[:, :].rearrange("p (t i) -> p t i", i=E)[:, a * HT:(a + 1) * HT, s * D:(s + 1) * D],
                    look_ps[(a * NSMALL + n) % 2][:, 0:HT * PARTS * D].rearrange("p (t c d) -> p t d c", t=HT, c=PARTS),
                    AX_X, ALU.add).then_inc(looked_up, 1)

            def lookup_step(a, i):
                make_onehot(a, i)
                n, c = LOOKUPS[i]
                if n > 0 and c == TAKE_AT:
                    take_rows(a, n - 1)

            def split_weights(i):
                dve.wait_ge(weights_high, i + 1)
                parts_of, weights = ((w1z_parts, w1z_sb), (w2_parts, w2_sb))[i]
                dve.tensor_tensor(parts_of[:, 1, :, :], weights[:, :, :], parts_of[:, 0, :, :],
                                  ALU.subtract).then_inc(weights_low, 1)

            def make_z_low(m, p):
                dve.wait_ge(z_ready, m + 1)
                dve.tensor_tensor(z_low, z_ps[p][:, :].rearrange("p (a b) -> p a b", a=2), z_high,
                                  ALU.subtract).then_inc(z_low_ready, 1)

            def make_h1_low(m, i):
                dve.wait_ge(h1_ready, 2 * m + (i + 1))
                dve.scalar_tensor_tensor(h1_low[:, 2 * i:2 * i + 2, :], h1_ps[i][:, :].rearrange("p (a b) -> p a b", a=2), 0.0,
                                         h1_high[:, 2 * i:2 * i + 2, :], ALU.max, ALU.subtract).then_inc(h1_low_ready, 1)

            dve.wait_ge(table_in, 16)
            split_tables(0, slice(0, FIRST_TABLES))
            dve.wait_ge(masks_in, 16)
            for i in range(NCHUNK):
                lookup_step(0, i)
                if i == SPLIT_AT:
                    dve.wait_ge(split_step, 4)
                    split_tables(1, slice(FIRST_TABLES, NCHUNK))
                if i == SUM_AT:
                    spread_alpha()
                if i == MULTIPLY_AT:
                    multiply_weights()
                if i == DENSE_AT:
                    split_dense()
            take_rows(0, NSMALL - 1)
            for i in late_lookups(-1):
                lookup_step(1, i)

            for g in range(GROUPS):
                p = g % 2
                dve.wait_ge(x0_in[p], 16 * X0_LOADS * (g // 2 + 1))
                for c in range(NC):
                    dve.wait_ge(xl_ready, XLP * g + (c // 2 + 1))
                    if g > 0:
                        dve.wait_ge(contracted, NC * (g - 1) + (c + 1))
                    x0 = x0_main if c < MC else x0_last
                    dve.tensor_tensor(prod[:, c, :, :], x0[:, p, :, :],
                                      xl[:, p, c, :].unsqueeze(1).broadcast_to([P, HP, GB]),
                                      ALU.mult).then_inc(product_ready, 1)
                    if NC * g + c > 0:
                        for i in late_lookups(NC * g + c - 1):
                            lookup_step(1, i)
                    if NC * g + c == LATE_STEPS:
                        take_rows(1, NSMALL - 1)
                    if g == SPLIT_FROM and c > ROUND_AT:
                        split_weights(c - ROUND_AT - 1)
                    if g > SPLIT_FROM and c == Z_LOW_AT:
                        make_z_low(g - 1, 1 - p)
                    for i in range(2):
                        if g > SPLIT_FROM and c == H1_LOW_AT[i]:
                            make_h1_low(g - 1, i)
            m, p = GROUPS - 1, (GROUPS - 1) % 2
            make_z_low(m, p)
            for i in range(2):
                make_h1_low(m, i)

        @block.tensor
        def _(pe):
            def sum_alpha():
                pe.wait_ge(prep_in, 16 * PREP_LOADS)
                pe.wait_ge(alpha_spread, 1)
                for c in range(F8):
                    last = pe.matmul(b_ps[c // 4][:, c % 4 * P:(c % 4 + 1) * P], mask_sb[:, c * P:(c + 1) * P],
                                     alpha_block[:, c, :, :].rearrange("p f k -> p (f k)"), start=True, stop=True)
                last.then_inc(bsum_done, 1)

            def make_coef(k):
                if k == 0:
                    pe.wait_ge(bsum_copied, 2)
                    pe.wait_ge(wblock_done, 1)
                    pe.wait_ge(blast_done, 1)
                for j in range(2):
                    for odd in range(2):
                        row = 64 * j + 32 * odd
                        pe.matmul(c_ps[row:row + FM, k * MC * HP:(k + 1) * MC * HP], bsum_sb[:, 0:FM, k],
                                  wblock[:, k, j::2, odd::2], start=True, stop=True)
                last = pe.matmul(c4_ps[:, k * H:(k + 1) * H], blast[:, k, :, :, :].rearrange("p h f j -> p (h f j)"),
                                 wh_sb[:, k, :], start=True, stop=True)
                if k == K - 1:
                    last.then_inc(c_done, 1)

            def look_up(a, i):
                n, c = LOOKUPS[i]
                at = a * NCHUNK + i
                turn = a * NSMALL + n
                if c == 0 and turn >= 2:
                    pe.wait_ge(looked_up, turn - 1)
                pe.wait_ge(onehot_ready, at + 1)
                for t in range(HT):
                    last = pe.matmul(look_ps[turn % 2][:, t * PARTS * D:(t + 1) * PARTS * D],
                                     onehot[:, at % SLOTS, t * P:(t + 1) * P],
                                     parts[:, i, :, :].rearrange("p c d -> p (c d)"),
                                     start=(c == 0 and t == 0), stop=(c == CHUNKS[n] - 1), skip_group_check=True)
                last.then_inc(onehot_used, 1)

            pe.wait_ge(split_step, 4)
            made = 0
            for i in range(NCHUNK):
                if i == FIRST_TABLES:
                    pe.wait_ge(split_step, 8)
                look_up(0, i)
                if i == SUM_AT:
                    sum_alpha()
                if i >= COEF_AT and (i - COEF_AT) % COEF_EVERY == 0 and made < K:
                    make_coef(made)
                    made += 1

            def transpose_values(g, p):
                pe.wait_ge(spread_ready, g + 1)
                for i in range(XLP):
                    if g > 0 or i >= 2:
                        pe.wait_ge(xl_ready, XLP * g + (i - 1))
                    for c in range(2 * i, min(2 * i + 2, NC)):
                        for t in range(TPG):
                            col = c % 2 * GB + t * P
                            last = pe.transpose(t_ps[(p + i) % 2][:, col:col + P],
                                                spread[:, p, t, c * P:(c + 1) * P], ident[:, :])
                    last.then_inc(transposed, 1)

            def contract(g, p, c):
                pe.wait_ge(product_ready, NC * g + (c + 1))
                for a in range(2):
                    for q in range(4):
                        last = pe.matmul(z_ps[p][32 * q:32 * q + 32, a * GB:(a + 1) * GB], coef[:, c, 4 * a + q, :],
                                         prod[:, c, 4 * a + q, :], start=(c == 0 and a == 0), stop=(c == NC - 1),
                                         skip_group_check=True)
                last.then_inc(contracted, 1)

            def high_products(out, weights, k, cols, high, first):
                pe.matmul(out, weights[:, 0, k, cols], high, start=first, stop=False, skip_group_check=True)
                pe.matmul(out, weights[:, 1, k, cols], high, start=False, stop=False, skip_group_check=True)

            def layer1(m, p, i):
                if 0 < m <= SPLIT_FROM and i == 0:
                    pe.wait_ge(y_ready, m)
                if m == SPLIT_FROM and i == 0:
                    pe.wait_ge(weights_low, 2)
                out = [h1_ps[i][:, a * GB:(a + 1) * GB] for a in range(2)]
                cols = [slice((2 * i + a) * P, (2 * i + a + 1) * P) for a in range(2)]
                for a in range(2):
                    pe.matmul(out[a], w1d_sb[:, cols[a]], dense_sb[:, m * GB:(m + 1) * GB], start=(a == 0), stop=False,
                              skip_group_check=True)
                if i == 0:
                    pe.wait_ge(z_ready, m + 1)
                if m < SPLIT_FROM:
                    for a in range(2):
                        for k in range(2):
                            last = pe.matmul(out[a], w1z_sb[:, k, cols[a]], z_sb[:, p, k, :], start=False, stop=(k == 1),
                                             skip_group_check=True)
                else:
                    for a in range(2):
                        for k in range(2):
                            high_products(out[a], w1z_parts, k, cols[a], z_high[:, k, :], False)
                    if i == 0:
                        pe.wait_ge(z_low_ready, m - SPLIT_FROM + 1)
                    for a in range(2):
                        for k in range(2):
                            last = pe.matmul(out[a], w1z_parts[:, 0, k, cols[a]], z_low[:, k, :], start=False, stop=(k == 1),
                                             skip_group_check=True)
                last.then_inc(h1_summed, 1)

            def layer2(m):
                out = [h2_ps(m)[:, a * GB:(a + 1) * GB] for a in range(2)]
                cols = [slice(a * P, (a + 1) * P) for a in range(2)]
                if m < SPLIT_FROM:
                    pe.wait_ge(h1_ready, 2 * m + 2)
                    for a in range(2):
                        for c in range(N1 // P):
                            last = pe.matmul(out[a], w2_sb[:, c, cols[a]], h1_sb[:, c, :], start=(c == 0),
                                             stop=(c == N1 // P - 1))
                else:
                    if m == SPLIT_FROM:
                        pe.wait_ge(looked_up, 2 * NSMALL)
                    for c in range(N1 // P):
                        if c % 2 == 0:
                            pe.wait_ge(h1_ready, 2 * m + (c // 2 + 1))
                        for a in range(2):
                            high_products(out[a], w2_parts, c, cols[a], h1_high[:, c, :], c == 0 and a == 0)
                    for c in range(N1 // P):
                        if c % 2 == 0:
                            pe.wait_ge(h1_low_ready, 2 * (m - SPLIT_FROM) + (c // 2 + 1))
                        for a in range(2):
                            last = pe.matmul(out[a], w2_parts[:, 0, c, cols[a]], h1_low[:, c, :], start=False,
                                             stop=(c == N1 // P - 1), skip_group_check=True)
                last.then_inc(h2_summed, 1)

            def layer3(m):
                pe.wait_ge(h2_ready, 2 * m + 2)
                if m > SPLIT_FROM:
                    pe.wait_ge(y_ready, m)
                for a in range(2):
                    for q in range(4):
                        last = pe.matmul(y_ps(m)[32 * q:32 * q + 1, 0:GB // 4], w3_sb[:, a:a + 1],
                                         h2_sb[:, a, q * (GB // 4):(q + 1) * (GB // 4)], start=(a == 0), stop=(a == 1))
                last.then_inc(y_summed, 1)

            for i in late_lookups(-1):
                look_up(1, i)
                if made < K:
                    make_coef(made)
                    made += 1
            pe.wait_ge(ident_done, 2)
            pe.wait_ge(mlp_in, 16 * MLP_LOADS)
            pe.wait_ge(dense_low, 4)
            transpose_values(0, 0)
            pe.wait_ge(coef_done, 1)
            for g in range(GROUPS):
                p = g % 2
                for c in range(NC):
                    if g < GROUPS - 1 and c == TRANSPOSES_AT:
                        transpose_values(g + 1, 1 - p)
                    contract(g, p, c)
                    for i in range(2):
                        if g > 0 and c == LAYER1_AT[i]:
                            layer1(g - 1, 1 - p, i)
                    if g > 0 and c == LAYER2_AT:
                        layer2(g - 1)
                    for i in late_lookups(NC * g + c):
                        look_up(1, i)
                if g > 0:
                    layer3(g - 1)
            m, p = GROUPS - 1, (GROUPS - 1) % 2
            layer1(m, p, 0)
            layer1(m, p, 1)
            layer2(m)
            layer3(m)


def kernel(dense_ctx, ids, r_x0, W_top1, b_top1, W_top2, b_top2, W_top3, L0_rec_w, L0_rec_alpha, L0_rec_hv, **tables):
    import numpy as _np
    import concourse.bacc as _bacc
    from concourse import mybir as _mybir
    from concourse.bass_utils import run_bass_kernel_spmd as _run

    flat = lambda a: _np.ascontiguousarray(_np.asarray(a))
    ids, w1, hv = flat(ids), flat(W_top1), flat(L0_rec_hv)
    slot_mask, masks = shape_constants()
    x0 = _np.zeros((B, FM + 8, H), _np.float32)
    x0[:, 0:F] = flat(r_x0)
    arrays = {
        "ids": ids,
        "ids_t": flat(ids[:, ONE_HOT].T),
        **{f"tbl_{s}": flat(tables[f"tbl_{s}"]) for s in GATHERED},
        "x0_g": flat(x0.reshape(GROUPS, GB, FM + 8, HP, 2).transpose(0, 4, 2, 3, 1).reshape(GROUPS, 2, FM + 8, HP * GB)),
        "small_tables": _np.concatenate([flat(tables[f"tbl_{s}"]).reshape(RC, -1) for s in ONE_HOT], 1),
        "dense_t": _np.concatenate([flat(dense_ctx).T, _np.ones((1, B), _np.float32)], 0),
        "alpha": _np.concatenate([flat(L0_rec_alpha), _np.zeros(((8 * F8 - F) * S, K), _np.float32)], 0),
        "w_hv": _np.concatenate([flat(L0_rec_w).transpose(2, 0, 1).reshape(D, K * H), hv[:, :, 0].T], 1),
        "w1z": flat(w1[:K * H].reshape(K, H, N1).transpose(1, 0, 2).reshape(K * H, N1)),
        "w1d": _np.concatenate([w1[K * H:], flat(b_top1)[None]], 0),
        "w2": flat(W_top2),
        "b2": flat(b_top2),
        "w3": flat(W_top3),
        "slot_mask": slot_mask,
        "masks": masks,
    }
    nc = _bacc.Bacc("TRN2", target_bir_lowering=False, num_devices=1)
    aps = {n: nc.dram_tensor(n, a.shape, _mybir.dt.from_np(a.dtype), kind="ExternalInput").ap() for n, a in arrays.items()}
    table_aps = {s: aps.pop(f"tbl_{s}") for s in GATHERED}
    y = nc.dram_tensor("y", (B, 1), _mybir.dt.float32, kind="ExternalOutput").ap()
    dlrm_tower(nc, tables=table_aps, y=y, **aps)
    return _run(nc, [arrays], core_ids=[0]).results[0]["y"]
```
